# Optimizing a Trainium2 kernel written in Bass

```python
import numpy as np
import jax
import jax.numpy as jnp

def _softmax(x, axis=-1):
    return jax.nn.softmax(x, axis=axis)

def _gelu(x):
    return jax.nn.gelu(x, approximate=True)

def _silu(x):
    return jax.nn.silu(x)

def _sigmoid(x):
    return jax.nn.sigmoid(x)

def _layernorm(x, axis=-1, eps=1e-05):
    m = jnp.mean(x, axis=axis, keepdims=True)
    v = jnp.var(x, axis=axis, keepdims=True)
    return (x - m) / jnp.sqrt(v + eps)

def _scatter_add(tgt, idx, src, axis=0):
    return tgt.at[idx].add(src)

def _segment_sum(src, seg, n):
    return jax.ops.segment_sum(src, seg, n)
kernel_name = 'mk_macaron_d4_jaxref_r8_ad53f2'

def setup_inputs(seed: int=0):
    np.random.seed(seed)
    _w = jnp.asarray

    def _L0_attn_setup():
        import jax, jax.numpy as jnp
        import numpy as np
        D_MODEL = 128
        SCALE = float(np.sqrt(D_MODEL))
        key = jax.random.key(seed)
        k1, k2, k3 = jax.random.split(key, 3)
        input_data = jax.random.normal(k1, (4, 256, D_MODEL), dtype=jnp.float32)
        qk = jax.random.normal(k2, (D_MODEL, D_MODEL), dtype=jnp.float32) / SCALE
        ov = jax.random.normal(k3, (D_MODEL, D_MODEL), dtype=jnp.float32) / SCALE
        return {'input_data': input_data, 'qk': qk, 'ov': ov}
    _L0_attn_in = _L0_attn_setup()

    def _L0_ffn_setup():
        import jax, jax.numpy as jnp
        import numpy as np
        key = jax.random.key(seed)
        k1, k2, k3, k4, k5 = jax.random.split(key, 5)
        d_in, d_out, r = (128, 128, 32)
        x = jax.random.normal(k1, (8, 1024, d_in), dtype=jnp.float32)
        W = jax.random.normal(k2, (d_out, d_in), dtype=jnp.float32) * (1.0 / np.sqrt(d_in))
        b = jax.random.normal(k3, (d_out,), dtype=jnp.float32) * 0.01
        V_r = jax.random.normal(k4, (d_in, r), dtype=jnp.float32) * (1.0 / np.sqrt(d_in))
        C = jax.random.normal(k5, (d_out, r), dtype=jnp.float32) * (1.0 / np.sqrt(r))
        return {'x': x, 'W': W, 'b': b, 'V_r': V_r, 'C': C}
    _L0_ffn_in = _L0_ffn_setup()

    def _L1_attn_setup():
        import jax, jax.numpy as jnp
        import numpy as np
        B, L, D = (4, 512, 128)
        NK, KD = (32, 64)
        NH = D // NK
        NORM_ORD_EPS = 0.0001

        def krylov(Lq, A, bvec, cvec):
            x = bvec[..., None]
            A_ = A
            done = Lq == 1
            while not done:
                l = x.shape[-1]
                if Lq - l <= l:
                    done = True
                    _x = x[..., :Lq - l]
                else:
                    _x = x
                _x = A_ @ _x
                x = jnp.concatenate([x, _x], axis=-1)
                if not done:
                    A_ = A_ @ A_
            return jnp.einsum('hnl,hn->hl', x, cvec)

        def companion_kernel(a, bvec, cvec, Lq):
            a_norm = jnp.sum(jnp.abs(a), axis=-1, keepdims=True)
            a_n = jnp.where(jnp.mean(jnp.abs(a_norm)) > NORM_ORD_EPS, a / a_norm, a)
            nk, kd = a.shape
            shift = jnp.zeros((nk, kd, kd), a.dtype).at[:, 1:, :-1].set(jnp.eye(kd - 1, dtype=a.dtype))
            A = shift.at[:, :, -1].add(a_n)
            return krylov(Lq, A, bvec, cvec)

        def fft_conv(u_bdl, k_dl):
            Lq = u_bdl.shape[-1]
            n = 2 * Lq
            u_f = jnp.fft.rfft(u_bdl, n=n)
            v_f = jnp.fft.rfft(k_dl[:, :Lq], n=n)
            y = jnp.fft.irfft(u_f * v_f[None], n=n)[..., :Lq]
            return y
        key = jax.random.key(seed)
        k1, k2, k3, k4 = jax.random.split(key, 4)
        return {'u': jax.random.normal(k1, (B, L, D), jnp.float32), 'a': jax.random.normal(k2, (NK, KD), jnp.float32), 'b': jax.random.normal(k3, (NK, KD), jnp.float32), 'c': jax.random.normal(k4, (NK, KD), jnp.float32)}
    _L1_attn_in = _L1_attn_setup()

    def _L1_ffn_setup():
        import jax, jax.numpy as jnp
        import numpy as np
        TOP_K = 2
        key = jax.random.key(seed)
        k1, k2, k3, k4 = jax.random.split(key, 4)
        B, T, D, H, E = (2, 256, 128, 256, 8)
        x = jax.random.normal(k1, (B, T, D), dtype=jnp.float32)
        w12 = jax.random.normal(k2, (E, 2 * H, D), dtype=jnp.float32) * D ** (-0.5)
        w3 = jax.random.normal(k3, (E, D, H), dtype=jnp.float32) * H ** (-0.5)
        gate_w = jax.random.normal(k4, (E, D), dtype=jnp.float32) * D ** (-0.5)
        return {'x': x, 'w12': w12, 'w3': w3, 'gate_w': gate_w}
    _L1_ffn_in = _L1_ffn_setup()

    def _L2_attn_setup():
        import jax, jax.numpy as jnp
        import numpy as np
        D_MODEL = 128
        NUM_HEADS = 16
        HEAD_DIM = D_MODEL // NUM_HEADS

        def _rope(x):
            B, H, T, d = x.shape
            pos = jnp.arange(T, dtype=x.dtype)[:, None]
            freq_seq = jnp.arange(d // 2, dtype=x.dtype)
            inv_freq = 1.0 / 10000.0 ** (freq_seq / (d // 2))
            ang = pos * inv_freq[None, :]
            sin = jnp.sin(ang)[None, None]
            cos = jnp.cos(ang)[None, None]
            x1, x2 = (x[..., :d // 2], x[..., d // 2:])
            return jnp.concatenate((x1 * cos - x2 * sin, x1 * sin + x2 * cos), axis=-1)
        key = jax.random.key(seed)
        ks = jax.random.split(key, 9)
        B, T = (2, 256)
        s = 1.0 / np.sqrt(D_MODEL)
        inp = {'x': jax.random.normal(ks[0], (B, T, D_MODEL), dtype=jnp.float32), 'Wq': jax.random.normal(ks[1], (D_MODEL, D_MODEL), dtype=jnp.float32) * s, 'bq': jnp.zeros((D_MODEL,), dtype=jnp.float32), 'Wk': jax.random.normal(ks[2], (D_MODEL, D_MODEL), dtype=jnp.float32) * s, 'bk': jnp.zeros((D_MODEL,), dtype=jnp.float32), 'Wv': jax.random.normal(ks[3], (D_MODEL, D_MODEL), dtype=jnp.float32) * s, 'bv': jnp.zeros((D_MODEL,), dtype=jnp.float32), 'Wo': jax.random.normal(ks[4], (D_MODEL, D_MODEL), dtype=jnp.float32) * s, 'bo': jnp.zeros((D_MODEL,), dtype=jnp.float32)}
        return inp
    _L2_attn_in = _L2_attn_setup()

    def _L2_ffn_setup():
        import jax, jax.numpy as jnp
        import numpy as np
        DIM = 128
        HIDDEN = 384
        SCALE = 1.0 / 127.0

        def _dequant(w_int, dtype):
            return w_int.astype(dtype) * jnp.asarray(SCALE, dtype)
        key = jax.random.key(seed)
        k_x, k_g, k_u, k_d = jax.random.split(key, 4)
        x = jax.random.normal(k_x, (4, 256, DIM), dtype=jnp.float32)
        w_gate = jax.random.randint(k_g, (HIDDEN, DIM), -127, 128, dtype=jnp.int32)
        w_up = jax.random.randint(k_u, (HIDDEN, DIM), -127, 128, dtype=jnp.int32)
        w_down = jax.random.randint(k_d, (DIM, HIDDEN), -127, 128, dtype=jnp.int32)
        return {'x': x, 'w_gate': w_gate, 'w_up': w_up, 'w_down': w_down}
    _L2_ffn_in = _L2_ffn_setup()

    def _L3_attn_setup():
        import jax, jax.numpy as jnp
        import numpy as np
        import math
        N_HEADS = 16
        ROPE_BASE = 10000.0

        def build_rope_cache(seq_len, head_dim):
            theta = ROPE_BASE ** (-jnp.arange(0, head_dim, 2, dtype=jnp.float32) / head_dim)
            seq = jnp.arange(seq_len, dtype=jnp.float32)
            freqs = jnp.einsum('i,j->ij', seq, theta)
            return (jnp.sin(freqs), jnp.cos(freqs))

        def apply_rope(x, sin, cos):
            sin = sin[None, :, None, :]
            cos = cos[None, :, None, :]
            x1, x2 = (x[..., ::2], x[..., 1::2])
            return jnp.concatenate([x1 * cos - x2 * sin, x1 * sin + x2 * cos], axis=-1)
        key = jax.random.key(seed)
        ks = jax.random.split(key, 6)
        B, T, C = (2, 256, 128)
        s = 1.0 / math.sqrt(C)
        return {'x': jax.random.normal(ks[0], (B, T, C), dtype=jnp.float32), 'Wq': jax.random.normal(ks[1], (C, C), dtype=jnp.float32) * s, 'bq': jnp.zeros((C,), dtype=jnp.float32), 'Wk': jax.random.normal(ks[2], (C, C), dtype=jnp.float32) * s, 'bk': jnp.zeros((C,), dtype=jnp.float32), 'Wv': jax.random.normal(ks[3], (C, C), dtype=jnp.float32) * s, 'bv': jnp.zeros((C,), dtype=jnp.float32), 'Wo': jax.random.normal(ks[4], (C, C), dtype=jnp.float32) * s, 'bo': jnp.zeros((C,), dtype=jnp.float32)}
    _L3_attn_in = _L3_attn_setup()

    def _L3_ffn_setup():
        import jax, jax.numpy as jnp
        import numpy as np
        B, S, D, H, F, E = (2, 128, 128, 16, 256, 8)
        HD = D // H

        def _ln(x, g, b, eps=1e-05):
            m = x.mean(-1, keepdims=True)
            v = ((x - m) ** 2).mean(-1, keepdims=True)
            return (x - m) / jnp.sqrt(v + eps) * g + b
        key = jax.random.key(seed)
        ks = jax.random.split(key, 12)
        rn = lambda k, shp, s=0.02: jax.random.normal(k, shp, jnp.float32) * s
        return {'src': jax.random.normal(ks[0], (B, S, D), jnp.float32), 'q_w': rn(ks[1], (D, D)), 'k_w': rn(ks[2], (D, D)), 'v_w': rn(ks[3], (D, D)), 'out_w': rn(ks[4], (D, D)), 'gate_w': rn(ks[5], (D, D)), 'gate_b': rn(ks[6], (D,)), 'scale_w': rn(ks[7], (H, HD)), 'n1_g': jnp.ones((D,), jnp.float32), 'n1_b': jnp.zeros((D,), jnp.float32), 'n2_g': jnp.ones((D,), jnp.float32), 'n2_b': jnp.zeros((D,), jnp.float32), 'moe_gate_w': rn(ks[8], (D, E)), 'moe_gate_b': jnp.zeros((E,), jnp.float32), 'w1': rn(ks[9], (E, D, F)), 'b1': jnp.zeros((E, F), jnp.float32), 'ln_g': jnp.ones((E, F), jnp.float32), 'ln_b': jnp.zeros((E, F), jnp.float32), 'w2': rn(ks[10], (E, F, D)), 'b2': jnp.zeros((E, D), jnp.float32), 'res_scale': jnp.ones((E,), jnp.float32)}
    _L3_ffn_in = _L3_ffn_setup()
    _d = {'L0_attn_input_data': _L0_attn_in['input_data'], 'L0_attn_qk': _L0_attn_in['qk'], 'L0_attn_ov': _L0_attn_in['ov'], 'L0_ffn_W': _L0_ffn_in['W'], 'L0_ffn_b': _L0_ffn_in['b'], 'L0_ffn_V_r': _L0_ffn_in['V_r'], 'L0_ffn_C': _L0_ffn_in['C'], 'L1_attn_a': _L1_attn_in['a'], 'L1_attn_b': _L1_attn_in['b'], 'L1_attn_c': _L1_attn_in['c'], 'L1_ffn_w12': _L1_ffn_in['w12'], 'L1_ffn_w3': _L1_ffn_in['w3'], 'L1_ffn_gate_w': _L1_ffn_in['gate_w'], 'L2_attn_Wq': _L2_attn_in['Wq'], 'L2_attn_bq': _L2_attn_in['bq'], 'L2_attn_Wk': _L2_attn_in['Wk'], 'L2_attn_bk': _L2_attn_in['bk'], 'L2_attn_Wv': _L2_attn_in['Wv'], 'L2_attn_bv': _L2_attn_in['bv'], 'L2_attn_Wo': _L2_attn_in['Wo'], 'L2_attn_bo': _L2_attn_in['bo'], 'L2_ffn_w_gate': _L2_ffn_in['w_gate'], 'L2_ffn_w_up': _L2_ffn_in['w_up'], 'L2_ffn_w_down': _L2_ffn_in['w_down'], 'L3_attn_Wq': _L3_attn_in['Wq'], 'L3_attn_bq': _L3_attn_in['bq'], 'L3_attn_Wk': _L3_attn_in['Wk'], 'L3_attn_bk': _L3_attn_in['bk'], 'L3_attn_Wv': _L3_attn_in['Wv'], 'L3_attn_bv': _L3_attn_in['bv'], 'L3_attn_Wo': _L3_attn_in['Wo'], 'L3_attn_bo': _L3_attn_in['bo'], 'L3_ffn_q_w': _L3_ffn_in['q_w'], 'L3_ffn_k_w': _L3_ffn_in['k_w'], 'L3_ffn_v_w': _L3_ffn_in['v_w'], 'L3_ffn_out_w': _L3_ffn_in['out_w'], 'L3_ffn_gate_w': _L3_ffn_in['gate_w'], 'L3_ffn_gate_b': _L3_ffn_in['gate_b'], 'L3_ffn_scale_w': _L3_ffn_in['scale_w'], 'L3_ffn_n1_g': _L3_ffn_in['n1_g'], 'L3_ffn_n1_b': _L3_ffn_in['n1_b'], 'L3_ffn_n2_g': _L3_ffn_in['n2_g'], 'L3_ffn_n2_b': _L3_ffn_in['n2_b'], 'L3_ffn_moe_gate_w': _L3_ffn_in['moe_gate_w'], 'L3_ffn_moe_gate_b': _L3_ffn_in['moe_gate_b'], 'L3_ffn_w1': _L3_ffn_in['w1'], 'L3_ffn_b1': _L3_ffn_in['b1'], 'L3_ffn_ln_g': _L3_ffn_in['ln_g'], 'L3_ffn_ln_b': _L3_ffn_in['ln_b'], 'L3_ffn_w2': _L3_ffn_in['w2'], 'L3_ffn_b2': _L3_ffn_in['b2'], 'L3_ffn_res_scale': _L3_ffn_in['res_scale']}
    _x0 = _d['L0_attn_input_data']
    _d['L0_attn_input_data'] = jax.random.normal(jax.random.fold_in(jax.random.key(seed), 1), (1, 2048, 128), dtype=_x0.dtype)
    del _x0
    return _d

def reference(L0_attn_input_data, L0_attn_qk, L0_attn_ov, L0_ffn_W, L0_ffn_b, L0_ffn_V_r, L0_ffn_C, L1_attn_a, L1_attn_b, L1_attn_c, L1_ffn_w12, L1_ffn_w3, L1_ffn_gate_w, L2_attn_Wq, L2_attn_bq, L2_attn_Wk, L2_attn_bk, L2_attn_Wv, L2_attn_bv, L2_attn_Wo, L2_attn_bo, L2_ffn_w_gate, L2_ffn_w_up, L2_ffn_w_down, L3_attn_Wq, L3_attn_bq, L3_attn_Wk, L3_attn_bk, L3_attn_Wv, L3_attn_bv, L3_attn_Wo, L3_attn_bo, L3_ffn_q_w, L3_ffn_k_w, L3_ffn_v_w, L3_ffn_out_w, L3_ffn_gate_w, L3_ffn_gate_b, L3_ffn_scale_w, L3_ffn_n1_g, L3_ffn_n1_b, L3_ffn_n2_g, L3_ffn_n2_b, L3_ffn_moe_gate_w, L3_ffn_moe_gate_b, L3_ffn_w1, L3_ffn_b1, L3_ffn_ln_g, L3_ffn_ln_b, L3_ffn_w2, L3_ffn_b2, L3_ffn_res_scale):

    def _L0_attn_ref(input_data, qk, ov):
        import jax, jax.numpy as jnp
        import numpy as np
        D_MODEL = 128
        SCALE = float(np.sqrt(D_MODEL))
        S = input_data.shape[1]
        scores = jnp.einsum('bsd,de,bte->bst', input_data, qk, input_data) / SCALE
        causal = jnp.tril(jnp.ones((S, S), dtype=bool))
        scores = jnp.where(causal, scores, -jnp.inf)
        attn = jax.nn.softmax(scores, axis=-1)
        return jnp.einsum('bst,btd,de->bse', attn, input_data, ov)

    def _L0_ffn_ref(x, W, b, V_r, C):
        import jax, jax.numpy as jnp
        import numpy as np
        base = jnp.einsum('bsd,od->bso', x, W) + b
        correction = jnp.einsum('bsr,or->bso', jnp.einsum('bsd,dr->bsr', x, V_r), C)
        return base + correction

    def _L1_attn_ref(u, a, b, c):
        import jax, jax.numpy as jnp
        import numpy as np
        B, L, D = (4, 512, 128)
        NK, KD = (32, 64)
        NH = D // NK
        NORM_ORD_EPS = 0.0001

        def krylov(Lq, A, bvec, cvec):
            x = bvec[..., None]
            A_ = A
            done = Lq == 1
            while not done:
                l = x.shape[-1]
                if Lq - l <= l:
                    done = True
                    _x = x[..., :Lq - l]
                else:
                    _x = x
                _x = A_ @ _x
                x = jnp.concatenate([x, _x], axis=-1)
                if not done:
                    A_ = A_ @ A_
            return jnp.einsum('hnl,hn->hl', x, cvec)

        def companion_kernel(a, bvec, cvec, Lq):
            a_norm = jnp.sum(jnp.abs(a), axis=-1, keepdims=True)
            a_n = jnp.where(jnp.mean(jnp.abs(a_norm)) > NORM_ORD_EPS, a / a_norm, a)
            nk, kd = a.shape
            shift = jnp.zeros((nk, kd, kd), a.dtype).at[:, 1:, :-1].set(jnp.eye(kd - 1, dtype=a.dtype))
            A = shift.at[:, :, -1].add(a_n)
            return krylov(Lq, A, bvec, cvec)

        def fft_conv(u_bdl, k_dl):
            Lq = u_bdl.shape[-1]
            n = 2 * Lq
            u_f = jnp.fft.rfft(u_bdl, n=n)
            v_f = jnp.fft.rfft(k_dl[:, :Lq], n=n)
            y = jnp.fft.irfft(u_f * v_f[None], n=n)[..., :Lq]
            return y
        Bq, Lq, Dq = u.shape
        nk = a.shape[0]
        nh = Dq // nk
        ut = jnp.swapaxes(u, 1, 2)
        k = companion_kernel(a, b, c, Lq)
        k_full = jnp.repeat(k, nh, axis=0)
        y = fft_conv(ut, k_full)
        return jnp.swapaxes(y, 1, 2)

    def _L1_ffn_ref(x, w12, w3, gate_w):
        import jax, jax.numpy as jnp
        import numpy as np
        TOP_K = 2
        E = gate_w.shape[0]
        H = w3.shape[-1]
        scores = jnp.einsum('btd,ed->bte', x, gate_w)
        topk_scores, topk_idx = jax.lax.top_k(scores, TOP_K)
        topk_probs = jax.nn.softmax(topk_scores, axis=-1)
        total_probs = jnp.sum(jax.nn.one_hot(topk_idx, E, dtype=topk_probs.dtype) * topk_probs[..., None], axis=-2)
        h12 = jnp.einsum('btd,ehd->bteh', x, w12)
        h1, h2 = (h12[..., :H], h12[..., H:])
        hidden = jax.nn.silu(h1) * h2
        expert_out = jnp.einsum('bteh,edh->bted', hidden, w3)
        y = jnp.sum(total_probs[..., None] * expert_out, axis=-2)
        return y

    def _L2_attn_ref(x, Wq, bq, Wk, bk, Wv, bv, Wo, bo):
        import jax, jax.numpy as jnp
        import numpy as np
        D_MODEL = 128
        NUM_HEADS = 16
        HEAD_DIM = D_MODEL // NUM_HEADS

        def _rope(x):
            B, H, T, d = x.shape
            pos = jnp.arange(T, dtype=x.dtype)[:, None]
            freq_seq = jnp.arange(d // 2, dtype=x.dtype)
            inv_freq = 1.0 / 10000.0 ** (freq_seq / (d // 2))
            ang = pos * inv_freq[None, :]
            sin = jnp.sin(ang)[None, None]
            cos = jnp.cos(ang)[None, None]
            x1, x2 = (x[..., :d // 2], x[..., d // 2:])
            return jnp.concatenate((x1 * cos - x2 * sin, x1 * sin + x2 * cos), axis=-1)
        B, T, _ = x.shape

        def proj(W, b):
            return (x @ W + b).reshape(B, T, NUM_HEADS, HEAD_DIM).transpose(0, 2, 1, 3)
        q = _rope(proj(Wq, bq))
        k = _rope(proj(Wk, bk))
        v = proj(Wv, bv)
        scores = jnp.einsum('bhqd,bhkd->bhqk', q, k) / jnp.sqrt(jnp.asarray(HEAD_DIM, dtype=x.dtype))
        attn = jax.nn.softmax(scores, axis=-1)
        ctx = jnp.einsum('bhqk,bhkd->bhqd', attn, v)
        ctx = ctx.transpose(0, 2, 1, 3).reshape(B, T, D_MODEL)
        return ctx @ Wo + bo

    def _L2_ffn_ref(x, w_gate, w_up, w_down):
        import jax, jax.numpy as jnp
        import numpy as np
        DIM = 128
        HIDDEN = 384
        SCALE = 1.0 / 127.0

        def _dequant(w_int, dtype):
            return w_int.astype(dtype) * jnp.asarray(SCALE, dtype)
        wg = _dequant(w_gate, x.dtype)
        wu = _dequant(w_up, x.dtype)
        wd = _dequant(w_down, x.dtype)
        gate = jnp.einsum('bsd,hd->bsh', x, wg)
        up = jnp.einsum('bsd,hd->bsh', x, wu)
        h = jax.nn.silu(gate) * up
        return jnp.einsum('bsh,dh->bsd', h, wd)

    def _L3_attn_ref(x, Wq, bq, Wk, bk, Wv, bv, Wo, bo):
        import jax, jax.numpy as jnp
        import numpy as np
        import math
        N_HEADS = 16
        ROPE_BASE = 10000.0

        def build_rope_cache(seq_len, head_dim):
            theta = ROPE_BASE ** (-jnp.arange(0, head_dim, 2, dtype=jnp.float32) / head_dim)
            seq = jnp.arange(seq_len, dtype=jnp.float32)
            freqs = jnp.einsum('i,j->ij', seq, theta)
            return (jnp.sin(freqs), jnp.cos(freqs))

        def apply_rope(x, sin, cos):
            sin = sin[None, :, None, :]
            cos = cos[None, :, None, :]
            x1, x2 = (x[..., ::2], x[..., 1::2])
            return jnp.concatenate([x1 * cos - x2 * sin, x1 * sin + x2 * cos], axis=-1)
        B, T, C = x.shape
        H = N_HEADS
        D = C // H
        q = (x @ Wq.T + bq).reshape(B, T, H, D)
        k = (x @ Wk.T + bk).reshape(B, T, H, D)
        v = (x @ Wv.T + bv).reshape(B, T, H, D)
        sin, cos = build_rope_cache(T, D)
        q = apply_rope(q, sin, cos)
        k = apply_rope(k, sin, cos)
        scores = jnp.einsum('bqhd,bkhd->bhqk', q, k) / math.sqrt(D)
        causal = jnp.tril(jnp.ones((T, T), dtype=bool))
        scores = jnp.where(causal[None, None], scores, -jnp.inf)
        probs = jax.nn.softmax(scores, axis=-1)
        out = jnp.einsum('bhqk,bkhd->bqhd', probs, v).reshape(B, T, C)
        return out @ Wo.T + bo

    def _L3_ffn_ref(src, q_w, k_w, v_w, out_w, gate_w, gate_b, scale_w, n1_g, n1_b, n2_g, n2_b, moe_gate_w, moe_gate_b, w1, b1, ln_g, ln_b, w2, b2, res_scale):
        import jax, jax.numpy as jnp
        import numpy as np
        B, S, D, H, F, E = (2, 128, 128, 16, 256, 8)
        HD = D // H

        def _ln(x, g, b, eps=1e-05):
            m = x.mean(-1, keepdims=True)
            v = ((x - m) ** 2).mean(-1, keepdims=True)
            return (x - m) / jnp.sqrt(v + eps) * g + b
        b, s, d = src.shape
        h = scale_w.shape[0]
        hd = d // h
        q = (src @ q_w).reshape(b, s, h, hd).transpose(0, 2, 1, 3)
        k = (src @ k_w).reshape(b, s, h, hd).transpose(0, 2, 1, 3)
        v = (src @ v_w).reshape(b, s, h, hd).transpose(0, 2, 1, 3)
        scores = jnp.einsum('bhqd,bhkd->bhqk', q, k) / np.float32(np.sqrt(hd))
        scale = jax.nn.sigmoid(jnp.einsum('bhsd,hd->bhs', q, scale_w)) * 2.0
        scores = scores * scale[..., None]
        aw = jax.nn.softmax(scores, axis=-1)
        out = jnp.einsum('bhqk,bhkd->bhqd', aw, v).transpose(0, 2, 1, 3).reshape(b, s, d)
        gate = jax.nn.sigmoid(out @ gate_w + gate_b)
        attn = out * gate @ out_w
        x = _ln(src + attn, n1_g, n1_b)
        xr = x.reshape(-1, d)
        n = xr.shape[0]
        logits = xr @ moe_gate_w + moe_gate_b
        top_v, top_i = jax.lax.top_k(logits, 2)
        wts = jax.nn.softmax(top_v, axis=-1)
        chosen = jnp.max(top_i, axis=-1)

        def expert(W1, B1, G, Bt, W2, B2, rsc):
            hh = xr @ W1 + B1
            hh = jax.nn.gelu(_ln(hh, G, Bt), approximate=False)
            return (hh @ W2 + B2) * rsc + xr
        outs = jax.vmap(expert)(w1, b1, ln_g, ln_b, w2, b2, res_scale)
        sel = jnp.take_along_axis(outs.transpose(1, 0, 2), chosen[:, None, None], axis=1)[:, 0]
        moe = sel * jnp.sum(wts, axis=-1, keepdims=True)
        return _ln(x + moe.reshape(b, s, d), n2_g, n2_b)
    x = L0_attn_input_data
    x = x + 0.5 * _L0_ffn_ref(_layernorm(x, axis=-1), L0_ffn_W, L0_ffn_b, L0_ffn_V_r, L0_ffn_C)
    x = x + _L0_attn_ref(_layernorm(x, axis=-1), L0_attn_qk, L0_attn_ov)
    x = x + 0.5 * _L0_ffn_ref(_layernorm(x, axis=-1), L0_ffn_W, L0_ffn_b, L0_ffn_V_r, L0_ffn_C)
    x = x + 0.5 * _L1_ffn_ref(_layernorm(x, axis=-1), L1_ffn_w12, L1_ffn_w3, L1_ffn_gate_w)
    x = x + _L1_attn_ref(_layernorm(x, axis=-1), L1_attn_a, L1_attn_b, L1_attn_c)
    x = x + 0.5 * _L1_ffn_ref(_layernorm(x, axis=-1), L1_ffn_w12, L1_ffn_w3, L1_ffn_gate_w)
    x = x + 0.5 * _L2_ffn_ref(_layernorm(x, axis=-1), L2_ffn_w_gate, L2_ffn_w_up, L2_ffn_w_down)
    x = x + _L2_attn_ref(_layernorm(x, axis=-1), L2_attn_Wq, L2_attn_bq, L2_attn_Wk, L2_attn_bk, L2_attn_Wv, L2_attn_bv, L2_attn_Wo, L2_attn_bo)
    x = x + 0.5 * _L2_ffn_ref(_layernorm(x, axis=-1), L2_ffn_w_gate, L2_ffn_w_up, L2_ffn_w_down)
    x = x + 0.5 * _L3_ffn_ref(_layernorm(x, axis=-1), L3_ffn_q_w, L3_ffn_k_w, L3_ffn_v_w, L3_ffn_out_w, L3_ffn_gate_w, L3_ffn_gate_b, L3_ffn_scale_w, L3_ffn_n1_g, L3_ffn_n1_b, L3_ffn_n2_g, L3_ffn_n2_b, L3_ffn_moe_gate_w, L3_ffn_moe_gate_b, L3_ffn_w1, L3_ffn_b1, L3_ffn_ln_g, L3_ffn_ln_b, L3_ffn_w2, L3_ffn_b2, L3_ffn_res_scale)
    x = x + _L3_attn_ref(_layernorm(x, axis=-1), L3_attn_Wq, L3_attn_bq, L3_attn_Wk, L3_attn_bk, L3_attn_Wv, L3_attn_bv, L3_attn_Wo, L3_attn_bo)
    x = x + 0.5 * _L3_ffn_ref(_layernorm(x, axis=-1), L3_ffn_q_w, L3_ffn_k_w, L3_ffn_v_w, L3_ffn_out_w, L3_ffn_gate_w, L3_ffn_gate_b, L3_ffn_scale_w, L3_ffn_n1_g, L3_ffn_n1_b, L3_ffn_n2_g, L3_ffn_n2_b, L3_ffn_moe_gate_w, L3_ffn_moe_gate_b, L3_ffn_w1, L3_ffn_b1, L3_ffn_ln_g, L3_ffn_ln_b, L3_ffn_w2, L3_ffn_b2, L3_ffn_res_scale)
    return x

_drawn_inputs = setup_inputs


def setup_inputs(seed=0):
    import zlib

    import numpy as np

    out = dict(_drawn_inputs(seed))
    spreads = {'L2_attn_bq': (0.0, 0.8),
     'L2_attn_bk': (0.0, 0.8),
     'L2_attn_bv': (0.0, 0.8),
     'L2_attn_bo': (0.0, 2.0),
     'L3_attn_bq': (0.0, 0.8),
     'L3_attn_bk': (0.0, 0.8),
     'L3_attn_bv': (0.0, 2.0),
     'L3_attn_bo': (0.0, 2.0),
     'L3_ffn_n1_g': (1.0, 0.6),
     'L3_ffn_n1_b': (0.0, 2.0),
     'L3_ffn_n2_g': (1.0, 0.6),
     'L3_ffn_n2_b': (0.0, 2.0),
     'L3_ffn_moe_gate_b': (0.0, 2.0),
     'L3_ffn_b1': (0.0, 2.0),
     'L3_ffn_ln_g': (1.0, 0.6),
     'L3_ffn_ln_b': (0.0, 2.0),
     'L3_ffn_b2': (0.0, 2.0),
     'L3_ffn_res_scale': (1.0, 0.6)}
    factors = {'L0_ffn_b': 3.325,
     'L2_attn_Wq': 8.0,
     'L2_attn_Wk': 8.0,
     'L2_attn_Wv': 8.0,
     'L2_attn_Wo': 8.0,
     'L3_attn_Wq': 8.0,
     'L3_attn_Wk': 8.0,
     'L3_attn_Wv': 8.0,
     'L3_attn_Wo': 8.0,
     'L3_ffn_q_w': 64.0,
     'L3_ffn_k_w': 64.0,
     'L3_ffn_v_w': 64.0,
     'L3_ffn_out_w': 64.0,
     'L3_ffn_gate_w': 64.0,
     'L3_ffn_gate_b': 64.0,
     'L3_ffn_scale_w': 64.0,
     'L3_ffn_moe_gate_w': 64.0,
     'L3_ffn_w1': 64.0,
     'L3_ffn_w2': 64.0}
    for name, (base, spread) in spreads.items():
        noise = np.random.default_rng([zlib.crc32(name.encode()), seed]).standard_normal(out[name].shape)
        drawn = base * np.exp(spread * noise) if base else spread * noise
        out[name] = jnp.asarray(drawn.astype(out[name].dtype))
    for name, factor in factors.items():
        out[name] = (out[name] * factor).astype(out[name].dtype)
    return out
```

```python
from contextlib import ExitStack

import numpy as np
import concourse.bass as bass
from concourse import mybir

F32 = mybir.dt.float32
BF16 = mybir.dt.bfloat16
I32 = mybir.dt.int32
U32 = mybir.dt.uint32
ALU = mybir.AluOpType
ACT = mybir.ActivationFunctionType
AX = mybir.AxisListType.X

P = 128
T = 2048
NT = T // P
CH = 512
NC = T // CH
TPC = CH // P
HEADS = 16
HD = P // HEADS
GH = 4
NG = HEADS // GH
SPLIT = 3
TERMS = SPLIT * SPLIT
KR = TERMS * HD
KM = KR + SPLIT
VW = 2 * HD
E = 8
H1 = 256
H2 = 384
NK = 32
KD = 64
CPK = P // NK
ONE_PAIR = float(np.array([0x3F803F80], np.uint32).view(np.float32)[0])
NEG = -1.0e30
EPS = 1e-5

EARLY = dict(ident=P, flip=P, mask_q=P, mask_k=P, qk=P, ov=P, w0T=P, b0=P, vrT=P, cT=P, gate1=E,
             wqkv2=3 * P, bqkv2=3 * P, wo2=P, bo2=P, cos2=NT * 16, sin2=NT * 16, iota=E,
             ka=KD, kab=KD, kc=NK)
LATE = dict(wqkv3=3 * P, bqkv3=3 * P, wo3=P, bo3=P, cos3=NT * 16, sin3=NT * 16,
            mqkv=3 * P, mout=P, mgate=P, mgateb=P, mscale=P, n1g=P, n1b=P, n2g=P, n2b=P,
            moeg=E, moeb=E, table=3 * H1 + P + 1)


def columns(names):
    at, out = 0, {}
    for name, n in names.items():
        out[name] = (at, at + n)
        at += n
    return out, at


EARLY_AT, EARLY_N = columns(EARLY)
LATE_AT, LATE_N = columns(LATE)


class Lane:

    def __init__(self, sem):
        self.sem, self.count, self.steps, self.waited = sem, 0, [], {}

    def wait(self, *tokens):
        for token in tokens:
            if token is None:
                continue
            sem, count = token
            if count > self.waited.get(id(sem), 0):
                self.waited[id(sem)] = count
                self.steps.append(lambda eng, s=sem, c=count: eng.wait_ge(s, c))

    def do(self, make, *after, mark=True):
        self.wait(*after)
        if not mark:
            self.steps.append(make)
            return None
        self.count += 1
        self.steps.append(lambda eng, m=make, s=self.sem: m(eng).then_inc(s, 1))
        return (self.sem, self.count)

    def last(self):
        return (self.sem, self.count) if self.count else None

    def dma(self, channel, out, in_, *after):
        self.wait(*after)
        channel[1] += 16
        self.steps.append(lambda eng, o=out, i=in_, s=channel[0]: eng.dma_start(o, i).then_inc(s, 16))
        return (channel[0], channel[1])


def build(nc, d, out, stages=range(12)):
    with ExitStack() as ctx:
        def sb(name, shape, dt=F32):
            return ctx.enter_context(nc.sbuf_tensor(name, shape, dt))

        def sem(name):
            return ctx.enter_context(nc.semaphore(name))

        X = sb("X", [P, NT, P])
        XN = sb("XN", [P, NT, P])
        XNT = sb("XNT", [P, T])
        CTX = sb("CTX", [P, NT, P])
        VA = sb("VA", [P, NT, HEADS, VW])
        ARENA = 24576
        arena = sb("arena", [P, ARENA])
        parts = sb("parts", [P, 2, SPLIT, T], BF16)
        early = sb("early", [P, max(EARLY_N, LATE_N)])
        IDB = sb("IDB", [P, P], BF16)
        MQB = sb("MQB", [P, P], BF16)
        MKB = sb("MKB", [P, P], BF16)
        WEFF = sb("WEFF", [P, P])
        stat = sb("stat", [P, NT, 6])
        mv = sb("mv", [P, NT, 2])
        sd = sb("sd", [P, NT])
        rs = sb("rs", [P, NT])
        eps = sb("eps", [P, 1])
        small = sb("small", [P, 16, NT])
        lg = sb("lg", [P, NT, E])
        top = sb("top", [P, NT, E])
        topi = sb("topi", [P, NT, E], U32)
        topf = sb("topf", [P, NT, E])
        prob = sb("prob", [P, NT, E])
        pm = sb("pm", [P, 2, 16, NC])
        mx = sb("mx", [P, 2, 16])
        mr = sb("mr", [P, 2, 16])
        nmb = sb("nmb", [P, 2, 3 * 16], BF16)
        mt = sb("mt", [48, 2, P], BF16)
        rd = sb("rd", [P, 16])
        spread = sb("spread", [P, NT, 96], BF16)
        spreadT = sb("spreadT", [96, T], BF16)
        pick = sb("pick", [E, E, P], BF16)
        tableb = sb("tableb", [96, 3 * H1 + P + 1], BF16)
        ps = ctx.enter_context(nc.psum_tensor("ps", [P, 8 * CH], F32))
        k_dram = nc.dram_tensor("k_dram", (NK, P + T), F32, kind="Internal").ap()

        parts_dram = nc.dram_tensor("parts_dram", (2, SPLIT, NG, HD, GH * T), BF16, kind="Internal").ap()
        m_dram = nc.dram_tensor("m_dram", (2, 48, P), BF16, kind="Internal").ap()

        def bank(b, n=1):
            return ps[:, b * CH:(b + n) * CH]

        V, S, M, G, Y = (Lane(sem(n)) for n in ("vector_done", "scalar_done", "tensor_done", "gpsimd_done", "sync_done"))
        lanes = (V, S, M, G, Y)

        def channel(name):
            return [sem(name), 0]

        ch_x, ch_early, ch_late, ch_out = (channel(n) for n in ("x_in", "early_in", "late_in", "x_out"))
        ch_w = channel("stage_weights_in")
        ch_k = channel("kernel_rows_out")
        ch_toep = [channel(f"toeplitz_in{i}") for i in range(8)]
        ch_gather = [channel(f"gather{i}") for i in range(2)]
        ch_mo = [channel(f"maxima_out{i}") for i in range(2)]
        ch_m = [channel(f"maxima_rows{i}") for i in range(2)]
        ch_parts = [channel(f"parts_out{i}") for i in range(NC)]

        def settle(*more):
            tokens = [lane.last() for lane in lanes]
            for lane in lanes:
                lane.wait(*tokens, *more)

        class Arena:
            def __init__(self, at=0):
                self.at = at

            def take(self, *shape):
                n = int(np.prod(shape))
                ap = arena[:, self.at:self.at + n]
                self.at += n
                assert self.at <= ARENA
                if len(shape) == 2:
                    ap = ap.rearrange("p (a b) -> p a b", a=shape[0])
                elif len(shape) == 3:
                    ap = ap.rearrange("p (a b c) -> p a b c", a=shape[0], b=shape[1])
                return ap

        def ep(name, rows=P):
            a, b = EARLY_AT[name]
            return early[0:rows, a:b]

        def lp(name, rows=P):
            a, b = LATE_AT[name]
            return early[0:rows, a:b]

        def bc(ap, n):
            return ap.unsqueeze(1).broadcast_to((ap.shape[0], n, ap.shape[1]))

        def bcl(ap, n):
            return ap.unsqueeze(len(ap.shape)).broadcast_to(tuple(ap.shape) + (n,))

        def tiles(ap, n=TPC):
            return ap.rearrange("p (a b) -> p a b", a=n)

        x_in = Y.dma(ch_x, X[:, :, :], d["x"].rearrange("(i p) d -> p i d", p=P))
        early_in = S.dma(ch_early, early[:, 0:EARLY_N], d["early"])
        eps_set = V.do(lambda e: e.memset(eps[:, :], EPS))
        const_set = [V.do(lambda e: e.tensor_copy(IDB[:, :], ep("ident")), early_in),
                     V.do(lambda e: e.tensor_copy(MQB[:, :], ep("mask_q"))),
                     V.do(lambda e: e.tensor_copy(MKB[:, :], ep("mask_k")))]
        IDF = sb("IDF", [P, P])
        iota = sb("iota", [P, E])
        V.do(lambda e: e.tensor_copy(IDF[:, :], ep("ident")))
        V.do(lambda e: e.tensor_copy(iota[:, :], ep("iota")))
        for lane in (V, S, M, G):
            lane.wait(x_in, early_in)
        spread_zero = G.do(lambda e: e.memset(spread[:, :, :], 0.0))
        V.do(lambda e: e.tensor_copy(pick[:, :, :], bcl(ep("ident", E)[:, 0:E], P)))

        def normalise(dst, src, then):
            made, root = [], None
            for c in range(NC + 1):
                before = root
                if c < NC:
                    span = range(TPC * c, TPC * c + TPC)
                    seen = [V.do(lambda e, i=i: e.bn_stats(stat[:, i, :], src[:, i, :])) for i in span]
                    for i in span:
                        done = V.do(lambda e, i=i: e.bn_aggr(mv[:, i, :], stat[:, i, :]), seen[i % TPC])
                    cols = slice(TPC * c, TPC * c + TPC)
                    root = S.do(lambda e, cols=cols: e.activation(sd[:, cols], mv[:, cols, 1], ACT.Sqrt, bias=eps[:, 0:1]),
                                done, eps_set)
                if c:
                    cols = slice(TPC * c - TPC, TPC * c)
                    t = V.do(lambda e, cols=cols: e.reciprocal(rs[:, cols], sd[:, cols]), before)
                    made += [V.do(lambda e, i=i: e.tensor_scalar(dst[:, i, :], src[:, i, :], mv[:, i, 0:1], rs[:, i:i + 1],
                                                                 ALU.subtract, ALU.mult), t)
                             for i in range(TPC * c - TPC, TPC * c)]
                    then(c - 1, made)
            return made

        def turn(dst, src, made, banks=(0, 1)):
            out, free = [], [None, None]
            for c in range(NC):
                b = banks[c % 2]
                for i in range(TPC * c, TPC * c + TPC):
                    t = M.do(lambda e, i=i, b=b: e.transpose(bank(b)[:, (i % TPC) * P:(i % TPC + 1) * P],
                                                             src[:, i, :], IDF[:, :]), made[i], free[c % 2])
                lane = (S, V)[c % 2]
                if lane is S:
                    t = S.do(lambda e, b=b, c=c: e.activation(dst[:, c * CH:(c + 1) * CH], bank(b), ACT.Copy), t)
                else:
                    t = V.do(lambda e, b=b, c=c: e.tensor_copy(dst[:, c * CH:(c + 1) * CH], bank(b)), t)
                free[c % 2] = t
                out.append(t)
            return out

        def norm_turn(then=None, between=None):
            turned = []

            def each(c, made):
                b = c % 2
                for i in range(TPC * c, TPC * c + TPC):
                    t = M.do(lambda e, i=i: e.transpose(bank(b)[:, (i % TPC) * P:(i % TPC + 1) * P], XN[:, i, :],
                                                        IDF[:, :]), made[i], turned[c - 2] if c > 1 else None)
                turned.append(S.do(lambda e: e.activation(XNT[:, c * CH:(c + 1) * CH], bank(b), ACT.Copy), t))
                if between and c:
                    between(c - 1, turned[c - 1])

            normalise(XN, X, each)
            if between:
                between(NC - 1, turned[-1])
            for c in range(NC if then else 0):
                then(c, turned[c])
            return turned

        def product_chunk(weights, c, ready, use, free, banks=(2, 3), lhs=XNT):
            b = banks[c % 2]
            for i in range(TPC * c, TPC * c + TPC):
                t = M.do(lambda e, i=i: e.matmul(bank(b)[:, (i % TPC) * P:(i % TPC + 1) * P], lhs[:, i * P:(i + 1) * P],
                                                 weights, start=True, stop=True), ready, free[c % 2])
            free[c % 2] = use(TPC * c, TPC, bank(b), t)

        def token_product(weights, ready, use, banks=(2, 3), lhs=XNT):
            free = [None, None]
            for c in range(NC):
                product_chunk(weights, c, ready[c], use, free, banks, lhs)

        def lowrank_weight():
            t = M.do(lambda e: e.matmul(bank(0)[:, 0:P], ep("vrT", 32), ep("cT", 32), start=True, stop=True))
            return V.do(lambda e: e.tensor_tensor(WEFF[:, :], bank(0)[:, 0:P], ep("w0T"), ALU.add), t)

        def lowrank_ffn():
            free = [None, None]

            def add(i0, n, acc, t):
                xs = X[:, i0:i0 + n, :]
                t = V.do(lambda e: e.scalar_tensor_tensor(xs, tiles(acc, n), 0.5, xs, ALU.mult, ALU.add), t)
                V.do(lambda e: e.scalar_tensor_tensor(xs, bc(ep("b0"), n), 0.5, xs, ALU.mult, ALU.add), t)
                return t

            norm_turn(lambda c, turned: product_chunk(WEFF[:, :], c, turned, add, free))
            settle()

        f32_parts = parts[:, :, :, :].rearrange("p w k t -> p (w k t)").bitcast(F32)
        f32_values = VA[:, :, :, :].rearrange("p i h d -> p (i h d)")
        kernels_out = []

        def wide_attention(background):
            a = Arena()
            QT = a.take(T)
            prow = [a.take(T) for _ in range(2)]
            pT = [a.take(T) for _ in range(2)]
            AT = a.take(T)
            scale = 1.0 / float(np.sqrt(P))
            turned = norm_turn()
            free, qt = [None, None], []
            for c in range(NC):
                t = M.do(lambda e, c=c: e.matmul(bank(2 + c % 2), ep("qk"), XNT[:, c * CH:(c + 1) * CH],
                                                 start=True, stop=True), turned[c], free[c % 2])
                t = S.do(lambda e, c=c: e.activation(QT[:, c * CH:(c + 1) * CH], bank(2 + c % 2), ACT.Copy), t)
                free[c % 2] = t
                qt.append(t)
            settle()
            exped = [None] * NT
            made = [None] * NT
            nm, rsum = small[:, 0, :], small[:, 1, :]
            tfree = [None, None]
            afree = None
            pfree = [None, None]
            tread = [None, None]
            nturn = 0

            scored = [None] * NT
            copies = [[] for _ in range(NT)]

            def scores(i):
                n = (i + 1) * P
                for k0 in range(0, n, CH):
                    w = min(CH, n - k0)
                    last = k0 + w == n
                    M.do(lambda e, k0=k0, w=w, last=last: e.matmul(
                        ps[:, k0:k0 + w], QT[:, i * P:(i + 1) * P], XNT[:, k0:k0 + w], start=True, stop=not last),
                        exped[i - 1] if i else None, mark=False)
                scored[i] = M.do(lambda e: e.matmul(ps[:, i * P:(i + 1) * P], IDB[:, :], MQB[:, :], start=False, stop=True))

            def softmax(i):
                n = (i + 1) * P
                t = V.do(lambda e: e.tensor_reduce(nm[:, i:i + 1], ps[:, 0:n], AX, ALU.max), scored[i])
                t = V.do(lambda e: e.tensor_scalar(nm[:, i:i + 1], nm[:, i:i + 1], -scale, None, ALU.mult), t)
                exped[i] = S.do(lambda e: e.activation(prow[i % 2][:, 0:n], ps[:, 0:n], ACT.Exp, bias=nm[:, i:i + 1],
                                                       scale=scale, accum_out=rsum[:, i:i + 1]), t, pfree[i % 2])

            def turns(i):
                def group(j0):
                    nonlocal nturn
                    k, b = nturn % 2, 4 + nturn % 2
                    m = min(TPC, i + 1 - j0)
                    for j in range(j0, j0 + m):
                        t = M.do(lambda e, j=j: e.transpose(bank(b)[:, (j - j0) * P:(j - j0 + 1) * P],
                                                            prow[i % 2][:, j * P:(j + 1) * P], IDF[:, :]),
                                 exped[i], tfree[k])
                    pfree[i % 2] = t
                    dst, src = pT[i % 2][:, j0 * P:(j0 + m) * P], bank(b)[:, 0:m * P]
                    if nturn % 2:
                        t = V.do(lambda e: e.tensor_copy(dst, src), t, tread[i % 2])
                    else:
                        t = S.do(lambda e: e.activation(dst, src, ACT.Copy), t, tread[i % 2])
                    tfree[k] = t
                    copies[i].append(t)
                    nturn += 1

                return [lambda j0=j0: group(j0) for j0 in range(0, i + 1, TPC)]

            def products(i):
                def group(j0):
                    nonlocal afree
                    for j in range(j0, min(j0 + TPC, i + 1)):
                        t = M.do(lambda e, j=j: e.matmul(bank(6)[:, 0:P], pT[i % 2][:, j * P:(j + 1) * P], XN[:, j, :],
                                                         start=j == 0, stop=j == i), copies[i][j // TPC], afree)
                    if j == i:
                        tread[i % 2] = t
                        r = V.do(lambda e: e.reciprocal(small[:, 2, i:i + 1], rsum[:, i:i + 1]), exped[i])
                        made[i] = V.do(lambda e: e.tensor_scalar(CTX[:, i, :], bank(6)[:, 0:P], small[:, 2, i:i + 1], None,
                                                                 ALU.mult), t, r)
                        afree = made[i]

                return [lambda j0=j0: group(j0) for j0 in range(0, i + 1, TPC)]

            scores(0)
            softmax(0)
            for i in range(NT + 1):
                turning = turns(i) if i < NT else []
                multiplying = products(i - 1) if i else []
                if i + 1 < NT:
                    scores(i + 1)
                for step in turning[:2]:
                    step()
                    next(background, None)
                if i + 1 < NT:
                    softmax(i + 1)
                order = []
                for k in range(max(len(turning) - 2, len(multiplying))):
                    order += multiplying[k:k + 1] + turning[2:][k:k + 1]
                for step in order:
                    step()
                    next(background, None)
            for _ in background:
                pass
            settle()
            turned = turn(AT, CTX, made)

            def add(i0, n, acc, t):
                xs = X[:, i0:i0 + n, :]
                return V.do(lambda e: e.tensor_tensor(xs, tiles(acc, n), xs, ALU.add), t)

            token_product(ep("ov"), turned, add, lhs=AT)
            settle()

        def conv_kernels():
            a = Arena(6 * T)
            R = 2 * NK
            chain = a.take(KD, KD + 1)
            HK = NK // 2
            K = a.take(KD, R)
            SQ = a.take(HK, NK)
            kout = a.take(HK, KD)
            zero = a.take(P)
            col = a.take(16)
            ones = a.take(R)
            an = a.take(KD)

            def square(ap, k):
                return ap[:, k * HK * KD:(k + 1) * HK * KD].rearrange("p (h n) -> p h n", h=HK)

            halves = [slice(KD * k, KD * (k + 1)) for k in range(2)]
            KT = f32_parts[:, 2 * HK * KD:2 * HK * KD + NK * KD].rearrange(
                "p (h n) -> p h n", h=NK)
            G2 = [square(f32_parts, k) for k in range(2)]
            T2 = [square(f32_values, k) for k in range(2)]
            B = bank(7)
            free = None
            turn_of = [0]

            def copy(dst, src, ready):
                turn_of[0] += 1
                if turn_of[0] % 2:
                    return S.do(lambda e: e.activation(dst, src, ACT.Copy), ready)
                return V.do(lambda e: e.tensor_copy(dst, src), ready)

            cleared = V.do(lambda e: e.memset(chain[0:R, :, 0:1], 0.0))
            z = V.do(lambda e: e.memset(zero[:, :], 0.0))
            o = V.do(lambda e: e.memset(ones[0:R, :], 1.0 / R))
            t = V.do(lambda e: e.tensor_reduce(col[0:R, 0:1], ep("ka", R), AX, ALU.add, apply_absolute_value=True))
            t = M.do(lambda e: e.matmul(B[0:R, 0:1], ones[0:R, :], col[0:R, 0:1], start=True, stop=True), t, o)
            yield
            t = V.do(lambda e: e.tensor_scalar(col[0:R, 1:2], B[0:R, 0:1], 0.0001, None, ALU.is_gt), t)
            t2 = V.do(lambda e: e.tensor_scalar(col[0:R, 2:3], col[0:R, 1:2], -1.0, 1.0, ALU.mult, ALU.add), t)
            t = V.do(lambda e: e.scalar_tensor_tensor(col[0:R, 3:4], col[0:R, 0:1], col[0:R, 1:2], col[0:R, 2:3],
                                                      ALU.mult, ALU.add), t, t2)
            t = V.do(lambda e: e.reciprocal(col[0:R, 4:5], col[0:R, 3:4]), t)
            t = V.do(lambda e: e.tensor_scalar(an[0:R, :], ep("ka", R), col[0:R, 4:5], None, ALU.mult), t)
            t = V.do(lambda e: e.tensor_copy(chain[0:NK, 0, 1:KD + 1], an[0:NK, :]), t, cleared)
            t = V.do(lambda e: e.tensor_copy(chain[NK:R, 0, 1:KD + 1], early[NK:R, EARLY_AT["kab"][0]:EARLY_AT["kab"][1]]), t)
            for j in range(1, KD):
                t = V.do(lambda e, j=j: e.scalar_tensor_tensor(
                    chain[0:R, j, 1:KD + 1], an[0:R, :], chain[0:R, j - 1, KD:KD + 1], chain[0:R, j - 1, 0:KD],
                    ALU.mult, ALU.add), t)
                if j % 3 == 0:
                    yield
            free = made = t
            for k in range(KD // 8):
                for j in range(8 * k, 8 * k + 8):
                    t = M.do(lambda e, j=j: e.transpose(B[0:KD, (j % 8) * R:(j % 8 + 1) * R], chain[0:R, j, 1:KD + 1],
                                                        IDF[0:R, 0:R]), made, free)
                free = copy(K[halves[0], 8 * k:8 * k + 8, :], tiles(B[0:KD, :], 8), t)
                twice = copy(K[halves[1], 8 * k:8 * k + 8, :], K[halves[0], 8 * k:8 * k + 8, :], free)
                yield
            for k in range(KD // 16):
                for n in range(16 * k, 16 * k + 16):
                    t = M.do(lambda e, n=n: e.transpose(B[0:KD, (n % 16) * NK:(n % 16 + 1) * NK], chain[0:NK, :, 1 + n],
                                                        IDF[0:NK, 0:NK]), free)
                free = copy(KT[halves[0], :, 16 * k:16 * k + 16].rearrange("p h n -> p n h"), tiles(B[0:KD, :], 16), t)
                twice = copy(KT[halves[1], :, 16 * k:16 * k + 16], KT[halves[0], :, 16 * k:16 * k + 16], free)
                yield
            M.wait(twice)
            for k, part in enumerate(halves):
                rows = S.do(lambda e, k=k, part=part: e.activation(SQ[part, :, 0], ep("kc", KD)[:, HK * k:HK * (k + 1)],
                                                                   ACT.Copy))
            M.wait(rows)
            n = 1
            while n < NK:
                if n == 1:
                    def power(k, h):
                        return K[halves[k], :, HK * k + h]

                    def power_t(k, h):
                        return KT[halves[k], HK * k + h, :]
                else:
                    g, gt = G2[n.bit_length() % 2], T2[n.bit_length() % 2]

                    def power(k, h, g=g):
                        return g[halves[k], h, :]

                    def power_t(k, h, gt=gt):
                        return gt[halves[k], h, :]
                for h in range(HK):
                    for k in range(2):
                        t = M.do(lambda e, h=h, k=k, n=n, power=power: e.matmul(
                            B[halves[k], h * n:(h + 1) * n], power(k, h), SQ[halves[k], h, 0:n], start=True, stop=True),
                            free, mark=h == HK - 1)
                free = copy(SQ[:, :, n:2 * n], tiles(B[:, 0:HK * n], HK), t)
                yield
                if 2 * n < NK:
                    dg, dt_ = G2[(2 * n).bit_length() % 2], T2[(2 * n).bit_length() % 2]
                    for q in range(2):
                        for lhs, rhs, dst in ((power_t, power, dg), (power, power_t, dt_)):
                            for h in range(8 * q, 8 * q + 8):
                                for k in range(2):
                                    t = M.do(lambda e, h=h, k=k, lhs=lhs, rhs=rhs: e.matmul(
                                        B[halves[k], (h % 8) * KD:(h % 8 + 1) * KD], lhs(k, h), rhs(k, h), start=True,
                                        stop=True), free, mark=h % 8 == 7)
                            free = copy(dst[:, 8 * q:8 * q + 8, :], tiles(B, 8), t)
                            yield
                n *= 2
            for q in range(2):
                for h in range(8 * q, 8 * q + 8):
                    for k in range(2):
                        t = M.do(lambda e, h=h, k=k: e.matmul(
                            B[KD * k:KD * k + NK, (h % 8) * KD:(h % 8 + 1) * KD], SQ[halves[k], h, :],
                            K[halves[k], :, NK + HK * k + h], start=True, stop=True), free, mark=h % 8 == 7)
                copied = [copy(kout[KD * k:KD * k + NK, 8 * q:8 * q + 8, :], tiles(B[KD * k:KD * k + NK, :], 8), t)
                          for k in range(2)]
                M.wait(*copied)
                Y.wait(*copied)
                yield
            Y.dma(ch_k, k_dram[:, 0:P], zero[0:NK, :], z)
            for k in range(2):
                stored = Y.dma(ch_k, k_dram[HK * k:HK * (k + 1), P:].rearrange("h (i j) -> i h j", j=KD),
                               kout[KD * k:KD * k + NK, :, :])
            kernels_out.append(stored)

        TOEP = T + P // 2
        RING, EARLY_TOEP = 8, 3
        toep_early = [f32_parts[:, 0:TOEP], f32_parts[:, TOEP:2 * TOEP],
                      f32_values[:, 0:TOEP]]
        toep_in, toep_read = [None] * NK, [None] * NK

        def load_toeplitz(h, tile):
            src = bass.AP(tensor=k_dram.tensor, offset=h * (P + T) + 1, ap=[[1, P // 2], [1, TOEP]])
            toep_in[h] = Y.dma(ch_toep[h % RING], tile[0:P // 2, :], src, toep_read[h - RING] if h >= RING else None)

        def convolution():
            a = Arena(EXPERTS)
            U = a.take(NK, 2 * NT * CPK)
            ys = [a.take(CH) for _ in range(2)]
            toep = toep_early + [a.take(TOEP) for _ in range(RING - EARLY_TOEP)]
            shifted = [None] * NK

            def shift(h):
                tile = toep[h % RING]
                if h % 2:
                    shifted[h] = S.do(lambda e: e.activation(tile[P // 2:P, 0:T], tile[0:P // 2, P // 2:TOEP], ACT.Copy),
                                      toep_in[h])
                else:
                    shifted[h] = V.do(lambda e: e.tensor_copy(tile[P // 2:P, 0:T], tile[0:P // 2, P // 2:TOEP]), toep_in[h])

            def load(h):
                load_toeplitz(h, toep[h % RING])

            for h in range(EARLY_TOEP, RING):
                load(h)
            half = NT * CPK
            z = G.do(lambda e: e.memset(U[:, :, 0:half], 0.0))
            made = normalise(XN, X, lambda c, made: None)
            for c in range(NC):
                t = M.do(lambda e, c=c: e.matmul(bank(4 + c), ep("flip"), XN[:, TPC * c:TPC * c + TPC, :], start=True,
                                                 stop=True), made[TPC * c + TPC - 1])
                u = V.do(lambda e, c=c: e.tensor_copy(
                    U[:, :, half + c * TPC * CPK:half + (c + 1) * TPC * CPK].rearrange("p h (j c) -> p h j c", c=CPK),
                    bank(4 + c).rearrange("p (j h c) -> p h j c", j=TPC, c=CPK)), t)
            for h in range(4):
                shift(h)
            for b in range(4):
                for pair in range(4 * b, 4 * b + 4):
                    for delta in range(NT):
                        for k in range(2):
                            h = 2 * pair + k
                            t = M.do(lambda e, h=h, k=k, delta=delta, pair=pair: e.matmul(
                                bank(pair // 4)[64 * k:64 * k + 64, (pair % 4) * P:(pair % 4 + 1) * P],
                                U[:, h, (NT - delta) * CPK:(NT - delta) * CPK + half],
                                toep[h % RING][:, delta * P:(delta + 1) * P], start=delta == 0, stop=delta == NT - 1),
                                shifted[h], toep_in[h], u, z, mark=delta == NT - 1)
                            if delta == NT - 1:
                                toep_read[h] = t
                    for h in (2 * pair, 2 * pair + 1):
                        if h + RING < NK:
                            load(h + RING)
                        if h + 4 < NK:
                            shift(h + 4)
                t = S.do(lambda e, b=b: e.activation(ys[b % 2][:, :], bank(b), ACT.Copy), t)
                for q in range(4):
                    t = M.do(lambda e, q=q, b=b: e.transpose(bank(4 + b)[:, q * P:(q + 1) * P],
                                                             ys[b % 2][:, q * P:(q + 1) * P], IDF[:, :]), t)
                xs = X[:, :, 32 * b:32 * b + 32].rearrange("p i (g c) -> p g i c", c=CPK)
                V.do(lambda e, b=b, xs=xs: e.tensor_tensor(
                    xs, bank(4 + b).rearrange("p (g i c) -> p g i c", g=8, i=NT), xs, ALU.add), t)
            settle()

        def turn_spread(made, first):
            out, free = [], [None, None]
            for c in range(NC):
                narrow = bank(first + c % 2).bitcast(BF16)[0:96, 0:CH]
                for i in range(TPC * c, TPC * c + TPC):
                    t = M.do(lambda e, i=i, narrow=narrow: e.transpose(narrow[:, (i % TPC) * P:(i % TPC + 1) * P],
                                                                       spread[:, i, :], IDB[:, :]), made, free[c % 2])
                free[c % 2] = t = S.do(lambda e, c=c, narrow=narrow: e.activation(spreadT[:, c * CH:(c + 1) * CH], narrow,
                                                                                  ACT.Copy), t)
                out.append(t)
            return out

        def route(logits_made, routed):
            best, found = [], []
            for i in range(NT):
                best.append(V.do(lambda e, i=i: e.max(top[:, i, :], lg[:, i, :]), *logits_made))
                if i % 4 == 3:
                    yield
            for i in range(NT):
                found.append(V.do(lambda e, i=i: e.max_index(topi[:, i, :], top[:, i, :], lg[:, i, :]), best[i]))
                if i % 2:
                    yield
            idx = V.do(lambda e: e.tensor_copy(topf[:, :, :], topi[:, :, :]), *found)
            df, ex, den, p0, p1 = (small[:, 3 + k, :] for k in range(5))
            t = V.do(lambda e: e.tensor_tensor(df, top[:, :, 1], top[:, :, 0], ALU.subtract))
            t = S.do(lambda e: e.activation(ex, df, ACT.Exp), t)
            yield
            t = V.do(lambda e: e.tensor_scalar(den, ex, 1.0, None, ALU.add), t)
            t = V.do(lambda e: e.reciprocal(p0, den), t)
            yield
            routed += [V.do(lambda e: e.tensor_tensor(p1, p0, ex, ALU.mult), t), idx, p0, p1]

        def logits_between(weights):
            def between(c, turned):
                for i in range(TPC * c, TPC * c + TPC):
                    M.do(lambda e, i=i: e.matmul(bank(2)[:, i * E:(i + 1) * E], XNT[:, i * P:(i + 1) * P], weights,
                                                 start=True, stop=True), turned)

            return between

        def hidden(W1, W2col, ready, chunk, dst, freed, si, tilesn, background=iter(())):
            done = []
            for k in range(tilesn):
                b = k % 2
                rhs = XNT[:, chunk * CH:(chunk + 1) * CH]
                t1 = M.do(lambda e, k=k, b=b: e.matmul(bank(b), W1(k), rhs, start=True, stop=True),
                          ready[chunk], freed["h1"][b])
                t2 = M.do(lambda e, k=k, b=b: e.matmul(bank(2 + b), W2col(k), rhs, start=True, stop=True),
                          freed["h2"][b])
                t = S.do(lambda e, b=b: e.activation(si[b], bank(b), ACT.Silu), t1, freed["h2"][b])
                freed["h1"][b] = t
                t = V.do(lambda e, k=k, b=b: e.tensor_tensor(dst[:, k, :], si[b], bank(2 + b), ALU.mult), t, t2,
                         freed["dst"][chunk % 2])
                freed["h2"][b] = t
                done.append(t)
                next(background, None)
            return done

        EXPERTS = E * 2 * H1 + 2 * E * P
        loaded_experts = []

        def experts():
            a = Arena()
            w12, w3 = a.take(E * 2 * H1), a.take(2 * E, P)
            if not loaded_experts:
                Y.dma(ch_w, w12, d["w12T"])
                loaded_experts.append(Y.dma(ch_w, w3, d["w3T"]))
            return w12, w3, loaded_experts[0]

        def expert_ffn():
            a = Arena(EXPERTS)
            w12, w3, w_in = experts()
            HT = [a.take(2 * E, CH) for _ in range(2)]
            si = [arena_tail[:, 0:CH], arena_tail[:, CH:2 * CH]]
            router = logits_between(ep("gate1"))
            turned = norm_turn(between=router)
            logits = []

            def keep(i0, n, acc, t):
                t = V.do(lambda e: e.tensor_copy(lg[:, i0:i0 + n, :], tiles(acc, n)), t)
                logits.append(t)
                return t

            keep(0, NT, bank(2)[:, 0:NT * E], M.last())
            weights = []

            def routing():
                routed = []
                yield from route(logits, routed)
                p1_made, idx, p0, p1 = routed
                it = iota[:, :].unsqueeze(1).broadcast_to((P, NT, E))
                t = V.do(lambda e: e.tensor_tensor(prob[:, :, :], it, bcl(topf[:, :, 0], E), ALU.is_equal), p1_made, idx)
                u = V.do(lambda e: e.tensor_tensor(lg[:, :, :], it, bcl(topf[:, :, 1], E), ALU.is_equal))
                yield
                t = V.do(lambda e: e.tensor_tensor(prob[:, :, :], prob[:, :, :], bcl(p0, E), ALU.mult), t)
                u = V.do(lambda e: e.tensor_tensor(lg[:, :, :], lg[:, :, :], bcl(p1, E), ALU.mult), u)
                yield
                t = V.do(lambda e: e.tensor_tensor(prob[:, :, :], prob[:, :, :], lg[:, :, :], ALU.add), t, u)
                weights.append(V.do(lambda e: e.tensor_scalar(prob[:, :, :], prob[:, :, :], 0.5, None, ALU.mult), t))

            steps = routing()
            M.wait(w_in, logits[0])
            freed = {"h1": [None] * 2, "h2": [logits[0]] * 2, "dst": [None] * 2}
            ofree = [None] * 4
            k = 0

            def down(c, made):
                nonlocal k
                for tt in range(TPC):
                    i = TPC * c + tt
                    add = None
                    for half in range(2):
                        b = 4 + k % 4
                        for q in range(4):
                            ex = 4 * half + q
                            for s in range(2):
                                t = M.do(lambda e, ex=ex, s=s, q=q, b=b, tt=tt: e.matmul(
                                    bank(b)[:, q * P:(q + 1) * P], HT[c % 2][:, 2 * ex + s, tt * P:(tt + 1) * P],
                                    w3[:, 2 * ex + s, :], start=s == 0, stop=s == 1),
                                    made[2 * ex + s], ofree[k % 4], mark=q == 3 and s == 1)
                        for q in range(4):
                            ex = 4 * half + q
                            add = V.do(lambda e, ex=ex, q=q, b=b, i=i: e.scalar_tensor_tensor(
                                X[:, i, :], bank(b)[:, q * P:(q + 1) * P], prob[:, i, ex:ex + 1], X[:, i, :],
                                ALU.mult, ALU.add), t, weights[0], add)
                        ofree[k % 4] = add
                        k += 1
                freed["dst"][c % 2] = t

            before = None
            for c in range(NC):
                made = hidden(lambda k: w12[:, (k // 2) * 2 * H1 + (k % 2) * P:(k // 2) * 2 * H1 + (k % 2 + 1) * P],
                              lambda k: w12[:, (k // 2) * 2 * H1 + H1 + (k % 2) * P:(k // 2) * 2 * H1 + H1 + (k % 2 + 1) * P],
                              turned, c, HT[c % 2], freed, si, 2 * E, steps)
                for _ in steps:
                    pass
                if before:
                    down(c - 1, before)
                before = made
            down(NC - 1, before)
            settle()

        def quantised_ffn():
            a = Arena()
            wi = a.take(3 * H2)
            wf = a.take(3 * H2)
            HT = [a.take(H2 // P, CH) for _ in range(2)]
            si = [a.take(CH) for _ in range(2)]
            w_in = Y.dma(ch_w, wi.bitcast(I32), d["wq"])
            turned = norm_turn()
            scaled = V.do(lambda e: e.tensor_scalar(wf, wi.bitcast(I32), 1.0 / 127.0, None, ALU.mult), w_in)
            M.wait(scaled)
            freed = {"h1": [turned[2], turned[3]], "h2": [None] * 2, "dst": [None] * 2}
            ofree = [None] * 2
            for c in range(NC):
                made = hidden(lambda k: wf[:, k * P:(k + 1) * P], lambda k: wf[:, H2 + k * P:H2 + (k + 1) * P],
                              turned, c, HT[c % 2], freed, si, H2 // P)
                b = 4 + c % 2
                for tt in range(TPC):
                    for k in range(H2 // P):
                        t = M.do(lambda e, k=k, tt=tt, b=b, c=c: e.matmul(
                            bank(b)[:, tt * P:(tt + 1) * P], HT[c % 2][:, k, tt * P:(tt + 1) * P],
                            wf[:, 2 * H2 + k * P:2 * H2 + (k + 1) * P], start=k == 0, stop=k == H2 // P - 1),
                            made[k], ofree[c % 2])
                freed["dst"][c % 2] = t
                xs = X[:, TPC * c:TPC * c + TPC, :]
                ofree[c % 2] = V.do(lambda e, b=b, xs=xs: e.scalar_tensor_tensor(xs, tiles(bank(b)), 0.5, xs,
                                                                                 ALU.mult, ALU.add), t)
            settle()

        QKV = arena[:, 16384:16384 + NT * 384].rearrange("p (i n) -> p i n", i=NT)
        ROT = arena[:, 4096:4096 + NT * 256].rearrange("p (i n) -> p i n", i=NT)
        rem = arena[:, 22528:22528 + 2 * CH].rearrange("p (a n) -> p a n", a=2)
        rot_t = [[arena[:, at:at + CH].rearrange("p (i g n) -> p i g n", i=TPC, g=2 * NG)
                  for at in range(12288 + 2048 * b, 12288 + 2048 * (b + 1), CH)] for b in range(2)]
        packed = arena[:, 0:16384].bitcast(BF16).rearrange("p (w s h t) -> p w s h t", w=2, s=2, h=GH)
        QP, KP = packed[:, 0], packed[:, 1]
        PB = arena[:, 16384:24576].rearrange("p (n a t) -> p n a t", n=8, a=2)
        EV = sb("EV", [P, 2, CH])
        arena_tail = EV[:, :, :].rearrange("p a b -> p (a b)")

        def gather_rows(g, t0, n, *after):
            slot = g % 2
            for a in range(SPLIT):
                rows = slice(SPLIT * HD * a, SPLIT * HD * (a + 1))
                for dst, which, first, step in ((QP, 0, a, 0), (KP, 1, 0, P * T)):
                    src = bass.AP(tensor=parts_dram.tensor,
                                  offset=(which * SPLIT + first) * P * T + g * HD * GH * T + t0,
                                  ap=[[step, SPLIT], [GH * T, HD], [T, GH], [1, n]])
                    t = Y.dma(ch_gather[slot], dst[rows, slot, :, t0:t0 + n], src, *after)
            return t

        def prepare(weights, bias, transform, src):
            sums = G.do(lambda e: e.memset(VA[:, :, :, HD:VW], 1.0))
            ones = G.do(lambda e: e.memset(arena[64:96, 8192:12288], ONE_PAIR), sums)
            G.wait(ones)
            qfree, tfree, rfree = [None, None], [None, None], [None, None]

            def project(c, turned):
                made = []
                for i in range(TPC * c, TPC * c + TPC):
                    acc = bank(2 + i % 2)[:, 0:3 * P]
                    t = M.do(lambda e, i=i, acc=acc: e.matmul(acc, XNT[:, i * P:(i + 1) * P], weights, start=True, stop=True),
                             turned, qfree[i % 2])
                    if bias is None:
                        t = V.do(lambda e, i=i, acc=acc: e.tensor_copy(QKV[:, i, :], acc), t)
                    else:
                        t = V.do(lambda e, i=i, acc=acc: e.tensor_tensor(QKV[:, i, :], acc, bias, ALU.add), t)
                    qfree[i % 2] = t
                    made.append(t)
                span = slice(TPC * c, TPC * c + TPC)
                S.do(lambda e: e.activation(VA[:, span, :, 0:HD], QKV[:, span, 2 * P:3 * P].rearrange(
                    "p i (h d) -> p i h d", d=HD), ACT.Copy), *made)
                return transform(c, span, made)

            def split(c, ready):
                for w in range(2):
                    b = w
                    for i in range(TPC * c, TPC * c + TPC):
                        t = M.do(lambda e, i=i, b=b, w=w: e.transpose(bank(4 + b)[:, (i % TPC) * P:(i % TPC + 1) * P],
                                                                      src[:, i, w * P:(w + 1) * P], IDF[:, :]),
                                 *ready, tfree[b])
                    hi, mid, lo = (parts[:, w, k, c * CH:(c + 1) * CH] for k in range(SPLIT))
                    t = S.do(lambda e, b=b, hi=hi: e.activation(hi, bank(4 + b), ACT.Copy), t)
                    t = V.do(lambda e, b=b, hi=hi: e.tensor_tensor(rem[:, b, :], bank(4 + b), hi, ALU.subtract), t, rfree[b])
                    tfree[b] = t
                    t = S.do(lambda e, b=b, mid=mid: e.activation(mid, rem[:, b, :], ACT.Copy), t)
                    t = (V, G)[w].do(lambda e, b=b, mid=mid, lo=lo: e.tensor_tensor(lo, rem[:, b, :], mid, ALU.subtract), t)
                    rfree[b] = t
                    dst = bass.AP(tensor=parts_dram.tensor, offset=w * SPLIT * P * T + c * CH,
                                  ap=[[T, P], [P * T, SPLIT], [1, CH]])
                    t = Y.dma(ch_parts[c], dst, parts[:, w, :, c * CH:(c + 1) * CH], t)
                return t

            ready, stored = [], []

            def store(c):
                stored.append(split(c, ready[c]))
                if c:
                    gather_rows(0, (c - 1) * CH, CH, ones, stored[c - 1])

            def each(c, turned):
                ready.append(project(c, turned))
                if c:
                    store(c - 1)

            norm_turn(each)
            store(NC - 1)
            return stored, gather_rows(0, (NC - 1) * CH, CH, stored[-1])

        def rope(cos, sin):
            half = GH * HD // 2
            x = QKV[:, :, 0:2 * P].rearrange("p i (g a n) -> p i g a n", a=2, n=half)
            r = ROT[:, :, :].rearrange("p i (g a n) -> p i g a n", a=2, n=half)
            shape = (P, TPC, 2 * NG, half)
            tread = [(), ()]

            def transform(c, span, made):
                x1, x2 = x[:, span, :, 0, :], x[:, span, :, 1, :]
                cs = cos.rearrange("p (i n) -> p i n", i=NT)[:, span, :].unsqueeze(2).broadcast_to(shape)
                sn = sin.rearrange("p (i n) -> p i n", i=NT)[:, span, :].unsqueeze(2).broadcast_to(shape)
                tmp, free = rot_t[c % 2], tread[c % 2]
                a0 = V.do(lambda e: e.tensor_tensor(tmp[0], x1, cs, ALU.mult), *made, *free)
                a1 = G.do(lambda e: e.tensor_tensor(tmp[1], x2, sn, ALU.mult), *made, *free)
                a2 = V.do(lambda e: e.tensor_tensor(tmp[2], x1, sn, ALU.mult))
                a3 = G.do(lambda e: e.tensor_tensor(tmp[3], x2, cs, ALU.mult))
                a4 = G.do(lambda e: e.tensor_tensor(r[:, span, :, 1, :], tmp[2], tmp[3], ALU.add), a2, a3)
                a5 = V.do(lambda e: e.tensor_tensor(r[:, span, :, 0, :], tmp[0], tmp[1], ALU.subtract), a0, a1)
                tread[c % 2] = (a4, a5)
                return a4, a5

            return transform

        def heads_attention(scale, causal, stored, first):
            gathered = [first] + [None] * (NG - 1)
            group_read = [None] * NG
            settle()
            ones = G.do(lambda e: e.memset(arena[64:96, 12288:16384], ONE_PAIR))
            zeroed = V.do(lambda e: e.memset(bank(4), 0.0))

            def gather(g):
                gathered[g] = gather_rows(g, 0, T, ones, group_read[g - 2] if g >= 2 else None, *stored)

            units = [(g, NC - 1 - c if g % 2 else c) for g in range(NG) for c in range(NC)]
            m_ready = [None] * len(units)
            mfree = [None] * 3
            pbfree = [None] * 8
            stfree = [None, None]
            avfree = [zeroed]
            evfree = [None, None]
            turns = 0

            def take():
                nonlocal turns
                turns += 1
                return turns % 3

            later = []

            def maxima(u):
                g, c = units[u]
                slot = g % 2
                steps = []
                for hh in range(GH):
                    for qt in range(TPC):
                        i = TPC * c + qt
                        for kc in range(c + 1 if causal else NC):
                            diag = causal and kc == c
                            w = (qt + 1) * P if diag else CH
                            steps.append((hh, qt, i, kc, diag, w))

                def run(step, final):
                    hh, qt, i, kc, diag, w = step
                    b = take()
                    t = M.do(lambda e: e.matmul(bank(5 + b)[:, 0:w], QP[0:KR, slot, hh, i * P:(i + 1) * P],
                                                KP[0:KR, slot, hh, kc * CH:kc * CH + w], start=True, stop=not diag),
                             gathered[g], mfree[b], mark=not diag)
                    if diag:
                        t = M.do(lambda e: e.matmul(bank(5 + b)[:, w - P:w], IDB[:, :], MQB[:, :], start=False, stop=True))
                    mfree[b] = t = V.do(lambda e: e.tensor_reduce(pm[:, u % 2, hh * TPC + qt, kc:kc + 1], bank(5 + b)[:, 0:w],
                                                                  AX, ALU.max), t)
                    if final:
                        finish(t)

                def finish(t):
                    n = c + 1 if causal else NC
                    k = u % 2
                    t = V.do(lambda e: e.tensor_reduce(mx[:, k, :], pm[:, k, :, 0:n], AX, ALU.max), t)
                    t = V.do(lambda e: e.tensor_scalar(nmb[:, k, 0:16], mx[:, k, :], -1.0, None, ALU.mult), t,
                             nmb_read[k])
                    t = V.do(lambda e: e.scalar_tensor_tensor(mr[:, k, :], mx[:, k, :], -1.0, nmb[:, k, 0:16],
                                                              ALU.mult, ALU.subtract), t)
                    t = V.do(lambda e: e.tensor_copy(nmb[:, k, 16:32], mr[:, k, :]), t)
                    t = V.do(lambda e: e.tensor_tensor(nmb[:, k, 32:48], mr[:, k, :], nmb[:, k, 16:32], ALU.subtract), t)

                    def rows(t=t):
                        b = take()
                        narrow = bank(5 + b).bitcast(BF16)[0:48, 0:P]
                        tr = M.do(lambda e: e.transpose(narrow, nmb[:, k, :], IDB[:, :]), t, mfree[b])
                        nmb_read[k] = tr
                        mfree[b] = cp = V.do(lambda e: e.tensor_copy(mt[:, k, :], narrow), tr, mt_read[k])
                        mt_read[k] = Y.dma(ch_mo[k], m_dram[k], mt[:, k, :], cp, m_ready[u - 2] if u >= 2 else None)
                        m_ready[u] = Y.dma(ch_m[k], QP[KR:KM, slot, :, c * CH:(c + 1) * CH],
                                           m_dram[k].rearrange("(a h q) t -> a h (q t)", a=SPLIT, h=GH), mt_read[k])
                    later.append([3, rows])

                return [lambda s=s, f=k == len(steps) - 1: run(s, f) for k, s in enumerate(steps)]

            nmb_read = [None, None]
            mt_read = [None, None]
            rd_read = [None]

            def tick(everything=False):
                for item in list(later):
                    item[0] -= 1
                    if item[0] <= 0 or everything:
                        later.remove(item)
                        item[1]()

            gather(1)
            for step in maxima(0):
                step()
            tick(True)

            def batches(c):
                n = TPC * (c + 1) if causal else NT
                return [(j, j + 1) for j in range(0, n, 2)]

            LEAD = 8
            pending = []
            pending_unit = 0
            starts = [0]
            for _, c in units:
                starts.append(starts[-1] + len(batches(c)) * GH)
            queued = []
            total, clock = 0, 0
            nst, npb, nev = 0, 0, 0
            waiting = None

            def values(items, g, c, u, last):
                for jj in range(2):
                    for j, hh, pb, off, t_exp in items[jj]:
                        t = M.do(lambda e, j=j, hh=hh, pb=pb, off=off, jj=jj: e.matmul(
                            bank(4)[32 * hh:32 * hh + VW, off:CH], VA[:, j, GH * g + hh, :], PB[:, pb, jj, off:CH],
                            start=j == 0, stop=last and jj == 1, tile_position=(0, 32 * hh)),
                            t_exp, avfree[0] if j == 0 else None)
                        if jj == 1:
                            pbfree[pb] = t
                    yield
                if last:
                    k = u % 2
                    cp = S.do(lambda e: e.activation(EV[:, k, :], bank(4), ACT.Copy), t, evfree[k])
                    avfree[0] = cp

                    def turn_out():
                        b = take()
                        turned = bank(5 + b)
                        for q in range(TPC):
                            tr = M.do(lambda e, q=q: e.transpose(turned[:, q * P:(q + 1) * P], EV[:, k, q * P:(q + 1) * P],
                                                                 IDF[:, :]), cp, mfree[b])
                        evfree[k] = tr
                        seen = turned.rearrange("p (n w) -> p n w", w=32)
                        r = V.do(lambda e: e.reciprocal(rd[:, :], seen[:, :, HD]), tr, rd_read[0])
                        mfree[b] = rd_read[0] = V.do(lambda e: e.tensor_tensor(
                            CTX[:, TPC * c:TPC * c + TPC, 32 * g:32 * g + 32].rearrange("p q (h d) -> p q h d", d=HD),
                            turned.rearrange("p (q h w) -> p q h w", q=TPC, h=GH)[:, :, :, 0:HD],
                            bcl(rd[:, :].rearrange("p (q h) -> p q h", q=TPC), HD), ALU.mult), r)
                    later.append([3, turn_out])

            for u, (g, c) in enumerate(units):
                slot = g % 2
                if u % NC == 0 and 1 <= g < NG - 1:
                    gather(g + 1)
                todo = batches(c)
                for bi, (j0, j1) in enumerate(todo):
                    items = ([], [])
                    for hh in range(GH):
                        k = nst % 2
                        nst += 1
                        pb = npb % 8
                        npb += 1
                        offs = [max(0, (j - TPC * c) * P) if causal else 0 for j in (j0, j1)]
                        while pending_unit < min(u + 2, len(units) - 1):
                            pending_unit += 1
                            pending += maxima(pending_unit)
                            queued.append((starts[pending_unit] - LEAD, total + len(pending)))
                        n = max([-(-(upto - total) // max(1, by - clock)) for by, upto in queued if upto > total] + [0])
                        total += n
                        clock += 1
                        for jj, j in enumerate((j0, j1)):
                            off = offs[jj]
                            diag = causal and j >= TPC * c
                            t = M.do(lambda e, j=j, jj=jj, off=off, hh=hh, k=k, diag=diag, slot=slot, c=c: e.matmul(
                                bank(2 * k + jj)[:, off:CH], KP[0:KM, slot, hh, j * P:(j + 1) * P],
                                QP[0:KM, slot, hh, c * CH + off:(c + 1) * CH], start=True, stop=not diag),
                                m_ready[u], stfree[k], gathered[g], mark=not diag)
                            if diag:
                                t = M.do(lambda e, jj=jj, off=off, k=k: e.matmul(
                                    bank(2 * k + jj)[:, off:off + P], IDB[:, :], MKB[:, :], start=False, stop=True))
                            for _ in range((n + 1) // 2 if jj == 0 else n // 2):
                                pending.pop(0)()
                        group_read[g] = t
                        if offs == [0, 0]:
                            t = S.do(lambda e, k=k, pb=pb: e.activation(
                                PB[:, pb, :, :], bank(2 * k, 2).rearrange("p (a t) -> p a t", a=2), ACT.Exp, scale=scale),
                                t, pbfree[pb])
                        else:
                            for jj in range(2):
                                t = S.do(lambda e, jj=jj, k=k, pb=pb, off=offs[jj]: e.activation(
                                    PB[:, pb, jj, off:CH], bank(2 * k + jj)[:, off:CH], ACT.Exp, scale=scale),
                                    t, pbfree[pb])
                        stfree[k] = t
                        items[0].append((j0, hh, pb, offs[0], t))
                        items[1].append((j1, hh, pb, offs[1], t))
                        if waiting is not None and hh in (1, 3):
                            next(waiting, None)
                        tick()
                    if waiting is not None:
                        for _ in waiting:
                            pass
                    waiting = values(items, g, c, u, bi == len(todo) - 1)
            for _ in waiting:
                pass
            tick(True)
            tick(True)
            settle()

        def project_out(weights, bias, into):
            turned = turn(XNT, CTX, [None] * NT)
            token_product(weights, turned, into)

        def rope_attention(wqkv, bqkv, wo, bo, cos, sin, causal):
            stored, first = prepare(wqkv, bqkv, rope(cos, sin), ROT)
            heads_attention(1.0 / float(np.sqrt(HD)), causal, stored, first)

            def add(i0, n, acc, t):
                xs = X[:, i0:i0 + n, :]
                t = V.do(lambda e: e.tensor_tensor(xs, tiles(acc, n), xs, ALU.add), t)
                V.do(lambda e: e.tensor_tensor(xs, xs, bc(bo, n), ALU.add), t)
                return t

            project_out(wo, bo, add)
            settle()

        def sigmoid(dst, src, ready):
            return S.do(lambda e: e.activation(dst, src, ACT.Sigmoid), ready)

        def gated_block():
            prod = arena[:, 4096:4096 + NT * P].rearrange("p (i n) -> p i n", i=NT)
            zs = arena[:, 6144:6144 + NT * HEADS].rearrange("p (i n) -> p i n", i=NT)

            def transform(c, span, made):
                t = V.do(lambda e: e.tensor_tensor(prod[:, span, :], QKV[:, span, 0:P], bc(lp("mscale"), TPC), ALU.mult), *made)
                z = zs[:, span, :].rearrange("p i n -> p (i n)")
                t = V.do(lambda e: e.tensor_reduce(z, prod[:, span, :].rearrange("p i (g d h) -> p (i g) h d", g=NG, h=GH),
                                                   AX, ALU.add), t)
                t = sigmoid(z, z, t)
                t = V.do(lambda e: e.tensor_scalar(z, z, 2.0, None, ALU.mult), t)
                z4 = z.rearrange("p (i g h) -> p i g h", g=NG, h=GH)
                for g in range(NG):
                    q4 = QKV[:, span, 32 * g:32 * g + 32].rearrange("p i (d h) -> p i d h", h=GH)
                    zb = z4[:, :, g, :].unsqueeze(2).broadcast_to((P, TPC, HD, GH))
                    u = V.do(lambda e, q4=q4, zb=zb: e.tensor_tensor(q4, q4, zb, ALU.mult), t)
                return [u]

            stored, first = prepare(lp("mqkv"), None, transform, QKV)
            heads_attention(1.0 / float(np.sqrt(HD)), False, stored, first)
            Y.dma(ch_w, arena[:, 0:E * H1], d["w1"])
            w_in = Y.dma(ch_w, arena[:, E * H1:2 * E * H1], d["w2"])

            gated, normed = [], []
            GO = arena[:, 6144:6144 + NT * P].rearrange("p (i n) -> p i n", i=NT)
            GT = arena[:, 8192:8192 + T]

            def gate(i0, n, acc, t):
                dst = GO[:, i0:i0 + n, :]
                t = V.do(lambda e: e.tensor_tensor(dst, tiles(acc, n), bc(lp("mgateb"), n), ALU.add), t)
                u = sigmoid(dst, dst, t)
                gated.extend([V.do(lambda e: e.tensor_tensor(dst, dst, CTX[:, i0:i0 + n, :], ALU.mult), u)] * n)
                return t

            project_out(lp("mgate"), None, gate)
            turned = turn(GT, GO, gated, banks=(4, 5))

            def add(i0, n, acc, t):
                t = V.do(lambda e: e.tensor_tensor(CTX[:, i0:i0 + n, :], tiles(acc, n), XN[:, i0:i0 + n, :],
                                                   ALU.add), t)
                seen = [V.do(lambda e, i=i: e.bn_stats(stat[:, i, :], CTX[:, i, :]), t) for i in range(i0, i0 + n)]
                for i in range(i0, i0 + n):
                    normed.append(V.do(lambda e, i=i: e.bn_aggr(mv[:, i, :], stat[:, i, :]), seen[i - i0]))
                return t

            token_product(lp("mout"), turned, add, banks=(6, 7), lhs=GT)
            root = S.do(lambda e: e.activation(sd[:, :], mv[:, :, 1], ACT.Sqrt, bias=eps[:, 0:1]), normed[-1])
            t = V.do(lambda e: e.reciprocal(rs[:, :], sd[:, :]), root)
            router, turned = logits_between(lp("moeg")), []
            for c in range(NC):
                span = range(TPC * c, TPC * c + TPC)
                halfway = [V.do(lambda e, i=i: e.scalar_tensor_tensor(XN[:, i, :], CTX[:, i, :], mv[:, i, 0:1], lp("n1g"),
                                                                      ALU.subtract, ALU.mult), t) for i in span]
                made = [V.do(lambda e, i=i: e.scalar_tensor_tensor(XN[:, i, :], XN[:, i, :], rs[:, i:i + 1], lp("n1b"),
                                                                   ALU.mult, ALU.add), u) for i, u in zip(span, halfway)]
                for i in span:
                    u = M.do(lambda e, i=i, c=c: e.transpose(bank(c % 2)[:, (i % TPC) * P:(i % TPC + 1) * P], XN[:, i, :],
                                                             IDF[:, :]), made[i % TPC], turned[c - 2] if c > 1 else None)
                turned.append(S.do(lambda e, c=c: e.activation(XNT[:, c * CH:(c + 1) * CH], bank(c % 2), ACT.Copy), u))
                if c:
                    router(c - 1, turned[c - 1])
            router(NC - 1, turned[-1])
            t = M.last()
            t = V.do(lambda e: e.tensor_tensor(lg[:, :, :], tiles(bank(2)[:, 0:NT * E], NT), bc(lp("moeb"), NT), ALU.add), t)
            routed = []
            for _ in route([t], routed):
                pass
            routed, idx, p0, p1 = routed
            wsum, chosen = small[:, 8, :], small[:, 9, :]
            t_w = V.do(lambda e: e.tensor_tensor(wsum, p0, p1, ALU.add), routed)
            t = V.do(lambda e: e.tensor_tensor(chosen, topf[:, :, 0], topf[:, :, 1], ALU.max), idx)
            t = V.do(lambda e: e.tensor_tensor(prob[:, :, :], iota[:, :].unsqueeze(1).broadcast_to((P, NT, E)),
                                               bcl(chosen, E), ALU.is_equal), t)
            a = Arena(2 * E * H1)
            w1 = arena[:, 0:E * H1]
            w2 = arena[:, E * H1:2 * E * H1].rearrange("p (k n) -> p k n", k=2)
            HS = a.take(NT, H1)
            TW = 2 * H1 + P + 1
            TS = a.take(NT, TW)
            masked = [a.take(E, CH), VA[:, :, :, :].rearrange("p i h d -> p (i h d)").rearrange("p (a b) -> p a b", a=E)]
            for part in range(SPLIT):
                t = V.do(lambda e, part=part: e.tensor_copy(spread[:, :, 32 * part:32 * part + E], prob[:, :, :]), t)
            weights = turn_spread(t, 4)
            settle(w_in)

            mask_made = [[None] * E for _ in range(NC)]
            chunk_read = [None] * NC
            bfree = [None, None]

            def mask(c, ex):
                t = M.do(lambda e: e.matmul(bank(ex % 2), pick[:, ex, :], spreadT[0:E, c * CH:(c + 1) * CH],
                                            start=True, stop=True), bfree[ex % 2])
                bfree[ex % 2] = mask_made[c][ex] = V.do(lambda e: e.tensor_tensor(
                    masked[c % 2][:, ex, :], bank(ex % 2), XNT[:, c * CH:(c + 1) * CH], ALU.mult),
                    t, chunk_read[c - 2] if c > 1 else None)

            for ex in range(E):
                mask(0, ex)
            hfree, tfree = [None] * 2, [None, None]
            for i in range(NT):
                c, k, tb = i // TPC, i % 2, 4 + 2 * (i % 2)
                token = spreadT[:, i * P:(i + 1) * P]
                at = (i % TPC) * P
                M.do(lambda e, k=k, token=token: e.matmul(bank(2 + k)[:, 0:H1], token, tableb[:, 0:H1], start=True,
                                                          stop=False), hfree[k], mark=False)
                for ex in range(E):
                    t = M.do(lambda e, ex=ex, k=k, at=at, c=c: e.matmul(
                        bank(2 + k)[:, 0:H1], masked[c % 2][:, ex, at:at + P], w1[:, ex * H1:(ex + 1) * H1],
                        start=False, stop=ex == E - 1), mask_made[c][ex], mark=ex == E - 1)
                chunk_read[c] = t
                hfree[k] = u = S.do(lambda e, i=i, k=k: e.activation(HS[:, i, :], bank(2 + k)[:, 0:H1], ACT.Copy), t)
                M.do(lambda e, tb=tb, token=token: e.matmul(bank(tb), token, tableb[:, H1:3 * H1], start=True, stop=True),
                     tfree[k], mark=False)
                t = M.do(lambda e, tb=tb, token=token: e.matmul(bank(tb + 1)[:, 0:P + 1], token, tableb[:, 3 * H1:],
                                                                start=True, stop=True))
                tfree[k] = S.do(lambda e, i=i, tb=tb: e.activation(TS[:, i, :], bank(tb, 2)[:, 0:TW], ACT.Copy), t)
                seen = V.do(lambda e, i=i: e.bn_stats(stat[:, i, :], HS[:, i, :]), u)
                aggregated = V.do(lambda e, i=i: e.bn_aggr(mv[:, i, :], stat[:, i, :]), seen)
                if c + 1 < NC:
                    for ex in (2 * (i % TPC), 2 * (i % TPC) + 1):
                        mask(c + 1, ex)
            root = S.do(lambda e: e.activation(sd[:, :], mv[:, :, 1], ACT.Sqrt, bias=eps[:, 0:1]), aggregated)
            ready = V.do(lambda e: e.reciprocal(rs[:, :], sd[:, :]), root, tfree[0], tfree[1])
            bread, ofree = [None, None], [None, None]
            HTt = [EV[:, 0, 0:2 * P], EV[:, 1, 0:2 * P]]
            htread = [None, None]
            gel = [None] * NT
            multiplied = [None] * NT

            def activate(i):
                hs, ts = HS[:, i, :], TS[:, i, :]

                def centre():
                    gel[i] = V.do(lambda e: e.scalar_tensor_tensor(hs, hs, mv[:, i, 0:1], ts[:, 0:H1], ALU.subtract,
                                                                   ALU.mult), ready)

                def scale():
                    t = V.do(lambda e: e.scalar_tensor_tensor(hs, hs, rs[:, i:i + 1], ts[:, H1:2 * H1], ALU.mult,
                                                              ALU.add), gel[i])
                    gel[i] = S.do(lambda e: e.activation(hs, hs, ACT.Gelu), t)

                return [centre, scale]

            def multiply(i):
                k = i % 2
                for s in range(2):
                    t = M.do(lambda e, s=s: e.transpose(bank(k)[:, s * P:(s + 1) * P], HS[:, i, s * P:(s + 1) * P],
                                                        IDF[:, :]), gel[i], bread[k])
                bread[k] = cp = S.do(lambda e: e.activation(HTt[k], bank(k)[:, 0:2 * P], ACT.Copy), t, htread[k])
                for half in range(2):
                    for s in range(2):
                        t = M.do(lambda e, s=s, half=half: e.matmul(
                            bank(2 + 2 * k + half), HTt[k][:, s * P:(s + 1) * P], w2[:, s, half * CH:(half + 1) * CH],
                            start=s == 0, stop=s == 1), cp, ofree[k])
                htread[k] = multiplied[i] = t

            def choose(i, others):
                k, ts, acc, dst = i % 2, TS[:, i, :], None, CTX[:, i, :]
                for ex in range(E):
                    src = ts[:, 2 * H1:2 * H1 + P] if ex == 0 else dst
                    acc = V.do(lambda e, ex=ex, src=src: e.scalar_tensor_tensor(
                        dst, bank(2 + 2 * k, 2)[:, ex * P:(ex + 1) * P], prob[:, i, ex:ex + 1], src, ALU.mult, ALU.add),
                        multiplied[i], acc)
                    if others:
                        others.pop(0)()
                ofree[k] = acc
                last = [acc]

                def follow(make):
                    last[0] = V.do(make, last[0])
                    return last[0]

                return [lambda: follow(lambda e: e.scalar_tensor_tensor(dst, dst, ts[:, TW - 1:TW], XN[:, i, :], ALU.mult,
                                                                        ALU.add)),
                        lambda: follow(lambda e: e.scalar_tensor_tensor(dst, dst, wsum[:, i:i + 1], XN[:, i, :], ALU.mult,
                                                                        ALU.add)),
                        lambda: follow(lambda e: e.bn_stats(stat[:, i, :], dst)),
                        lambda: follow(lambda e: e.bn_aggr(mv[:, i, :], stat[:, i, :]))]

            for step in activate(0) + activate(1):
                step()
            multiply(0)
            after = []
            for i in range(NT):
                if i + 1 < NT:
                    multiply(i + 1)
                more = activate(i + 2) if i + 2 < NT else []
                order = [step for pair in zip(after, more + [None] * 4) for step in pair if step] if after else more
                after = choose(i, order)
            for step in after:
                done = step()
            root = S.do(lambda e: e.activation(sd[:, :], mv[:, :, 1], ACT.Sqrt, bias=eps[:, 0:1]), done)
            t = V.do(lambda e: e.reciprocal(rs[:, :], sd[:, :]), root)
            for c in range(NC):
                span = range(TPC * c, TPC * c + TPC)
                half = [V.do(lambda e, i=i: e.scalar_tensor_tensor(XN[:, i, :], CTX[:, i, :], mv[:, i, 0:1], lp("n2g"),
                                                                   ALU.subtract, ALU.mult), t) for i in span]
                u = [V.do(lambda e, i=i: e.scalar_tensor_tensor(XN[:, i, :], XN[:, i, :], rs[:, i:i + 1], lp("n2b"),
                                                                ALU.mult, ALU.add), w) for i, w in zip(span, half)]
                xs, ns = X[:, TPC * c:TPC * c + TPC, :], XN[:, TPC * c:TPC * c + TPC, :]
                V.do(lambda e, xs=xs, ns=ns: e.scalar_tensor_tensor(xs, ns, 0.5, xs, ALU.mult, ALU.add), *u)
            settle()

        late = []

        def load_late():
            if not late:
                settle()
                late.append(Y.dma(ch_late, early[:, 0:LATE_N], d["late"]))
                settle(late[0])
                rest = arena[0:E, 0:tableb.shape[1]]
                table = lp("table", E)
                zeroed = G.do(lambda e: e.memset(tableb[:, :], 0.0))
                t = V.do(lambda e: e.tensor_copy(tableb[0:E, :], table), zeroed)
                t = V.do(lambda e: e.tensor_tensor(rest, table, tableb[0:E, :], ALU.subtract), t)
                t = V.do(lambda e: e.tensor_copy(tableb[32:32 + E, :], rest), t)
                t = V.do(lambda e: e.tensor_tensor(tableb[64:64 + E, :], rest, tableb[32:32 + E, :], ALU.subtract), t)
                settle()

        settle()
        if any(s in stages for s in (0, 2)):
            lowrank_weight()
            settle()
        def early_toeplitz():
            settle(*kernels_out)
            for h in range(EARLY_TOEP):
                load_toeplitz(h, toep_early[h])

        if 4 in stages and 1 not in stages:
            for _ in conv_kernels():
                pass
            early_toeplitz()
        for s in stages:
            if s in (0, 2):
                if s == 2 and 3 in stages:
                    experts()
                lowrank_ffn()
            elif s == 1:
                wide_attention(conv_kernels() if 4 in stages else iter(()))
                if 4 in stages:
                    early_toeplitz()
            elif s in (3, 5):
                expert_ffn()
            elif s == 4:
                convolution()
            elif s in (6, 8):
                quantised_ffn()
            elif s == 7:
                rope_attention(ep("wqkv2"), ep("bqkv2"), ep("wo2"), ep("bo2"), ep("cos2"), ep("sin2"), False)
            elif s in (9, 11):
                load_late()
                gated_block()
            elif s == 10:
                load_late()
                rope_attention(lp("wqkv3"), lp("bqkv3"), lp("wo3"), lp("bo3"), lp("cos3"), lp("sin3"), True)
        stored = Y.dma(ch_out, out.rearrange("(i p) d -> p i d", p=P), X[:, :, :])
        Y.wait(stored)

        block = ctx.enter_context(nc.Block())
        for lane, engine in ((V, block.vector), (S, block.scalar), (M, block.tensor), (G, block.gpsimd), (Y, block.sync)):
            def program(eng, lane=lane):
                for step in lane.steps:
                    step(eng)
            engine(program)


def pack(names, arrays):
    total = sum(names.values())
    out = np.zeros((P, total), np.float32)
    at = 0
    for name, n in names.items():
        a = arrays[name]
        assert a.shape[1] == n, name
        out[:a.shape[0], at:at + n] = a
        at += n
    return out


def constants():
    f = np.float32
    q, k = np.meshgrid(np.arange(P), np.arange(P), indexing="ij")
    pos = np.arange(T, dtype=f)
    seq = np.arange(HD // 2, dtype=f)
    inv2 = (f(1.0) / np.power(f(10000.0), seq / f(HD // 2))).astype(f)
    ang2 = pos[:, None] * inv2[None, :]
    theta = np.power(f(10000.0), -np.arange(0, HD, 2, dtype=f) / f(HD)).astype(f)
    ang3 = pos[:, None] * theta[None, :]

    def tile(a):
        a = np.repeat(a.astype(f), GH, axis=1)
        return a.reshape(NT, P, GH * HD // 2).transpose(1, 0, 2).reshape(P, NT * GH * HD // 2)

    return dict(ident=np.eye(P, dtype=f), flip=np.eye(P, dtype=f)[::-1], mask_q=np.where(k > q, f(NEG), f(0)), mask_k=np.where(q > k, f(NEG), f(0)),
                iota=np.tile(np.arange(E, dtype=f), (P, 1)), cos2=tile(np.cos(ang2)), sin2=tile(np.sin(ang2)),
                cos3=tile(np.cos(ang3)), sin3=tile(np.sin(ang3)))


def by_group(a, pairs=False):
    a = np.asarray(a)
    lead = a.shape[:-1]
    a = a.reshape(lead + (NG, GH, HD))
    if pairs:
        a = np.concatenate([a[..., 0::2], a[..., 1::2]], -1)
    return np.swapaxes(a, -1, -2).reshape(lead + (P,))


def layout(i):
    c = constants()

    def rep(a):
        return np.broadcast_to(np.asarray(a).reshape(1, -1), (P, np.asarray(a).size))

    cat = np.concatenate
    early = dict(c)
    early.update(qk=i["L0_attn_qk"], ov=i["L0_attn_ov"], w0T=i["L0_ffn_W"].T, b0=rep(i["L0_ffn_b"]),
                 vrT=i["L0_ffn_V_r"].T, cT=i["L0_ffn_C"].T, gate1=i["L1_ffn_gate_w"].T,
                 wqkv2=cat([by_group(i["L2_attn_Wq"]), by_group(i["L2_attn_Wk"]), i["L2_attn_Wv"]], 1),
                 bqkv2=rep(cat([by_group(i["L2_attn_bq"]), by_group(i["L2_attn_bk"]), i["L2_attn_bv"]])),
                 wo2=i["L2_attn_Wo"], bo2=rep(i["L2_attn_bo"]),
                 ka=cat([i["L1_attn_a"], i["L1_attn_a"]], 0), kab=cat([i["L1_attn_b"], i["L1_attn_b"]], 0),
                 kc=i["L1_attn_c"].T)
    late = dict(c)
    late.update(wqkv3=cat([by_group(i["L3_attn_Wq"].T, True), by_group(i["L3_attn_Wk"].T, True), i["L3_attn_Wv"].T], 1),
                bqkv3=rep(cat([by_group(i["L3_attn_bq"], True), by_group(i["L3_attn_bk"], True), i["L3_attn_bv"]])),
                wo3=i["L3_attn_Wo"].T, bo3=rep(i["L3_attn_bo"]),
                mqkv=cat([by_group(i["L3_ffn_q_w"]), by_group(i["L3_ffn_k_w"]), i["L3_ffn_v_w"]], 1), mout=i["L3_ffn_out_w"],
                mgate=i["L3_ffn_gate_w"], mgateb=rep(i["L3_ffn_gate_b"]), mscale=rep(by_group(i["L3_ffn_scale_w"].reshape(P))),
                n1g=rep(i["L3_ffn_n1_g"]), n1b=rep(i["L3_ffn_n1_b"]), n2g=rep(i["L3_ffn_n2_g"]),
                n2b=rep(i["L3_ffn_n2_b"]), moeg=i["L3_ffn_moe_gate_w"], moeb=rep(i["L3_ffn_moe_gate_b"]),
                table=cat([i["L3_ffn_b1"], i["L3_ffn_ln_g"], i["L3_ffn_ln_b"], i["L3_ffn_b2"],
                           i["L3_ffn_res_scale"].reshape(E, 1)], 1))
    wd = i["L2_ffn_w_down"].T.reshape(H2 // P, P, P).transpose(1, 0, 2).reshape(P, H2)
    return {
        "x": i["L0_attn_input_data"].reshape(T, P),
        "early": pack(EARLY, early), "late": pack(LATE, late),
        "w12T": i["L1_ffn_w12"].transpose(2, 0, 1).reshape(P, E * 2 * H1),
        "w3T": i["L1_ffn_w3"].transpose(0, 2, 1).reshape(2 * E, P, P).transpose(1, 0, 2).reshape(P, 2 * E * P),
        "wq": cat([i["L2_ffn_w_gate"].T, i["L2_ffn_w_up"].T, wd], 1),
        "w1": i["L3_ffn_w1"].transpose(1, 0, 2).reshape(P, E * H1),
        "w2": i["L3_ffn_w2"].reshape(E, 2, P, P).transpose(2, 1, 0, 3).reshape(P, 2 * E * P),
    }


def kernel(**inputs):
    import concourse.bacc as bacc
    from concourse.bass_utils import run_bass_kernel_spmd

    arrays = {k: np.ascontiguousarray(v) for k, v in layout({k: np.asarray(v) for k, v in inputs.items()}).items()}
    nc = bacc.Bacc("TRN2", target_bir_lowering=False, num_devices=1)
    aps = {k: nc.dram_tensor(f"in_{k}", v.shape, mybir.dt.from_np(v.dtype), kind="ExternalInput").ap()
           for k, v in arrays.items()}
    out = nc.dram_tensor("out_x", (T, P), F32, kind="ExternalOutput").ap()
    build(nc, aps, out)
    r = run_bass_kernel_spmd(nc, [{f"in_{k}": v for k, v in arrays.items()}], core_ids=[0])
    return r.results[0]["out_x"].reshape(1, T, P)
```
